# Optimizing a Trainium2 kernel written in Bass

```python
import numpy as np
import jax
import jax.numpy as jnp

def _softmax(x, axis=-1):
    return jax.nn.softmax(x, axis=axis)

def _gelu(x):
    return jax.nn.gelu(x, approximate=True)

def _silu(x):
    return jax.nn.silu(x)

def _sigmoid(x):
    return jax.nn.sigmoid(x)

def _layernorm(x, axis=-1, eps=1e-05):
    m = jnp.mean(x, axis=axis, keepdims=True)
    v = jnp.var(x, axis=axis, keepdims=True)
    return (x - m) / jnp.sqrt(v + eps)

def _scatter_add(tgt, idx, src, axis=0):
    return tgt.at[idx].add(src)

def _segment_sum(src, seg, n):
    return jax.ops.segment_sum(src, seg, n)
kernel_name = 'mk_audio_tower_d1_tok_audfeat512_r4_913191'

def setup_inputs(seed: int=0):
    np.random.seed(seed)
    _w = jnp.asarray

    def _rec_inputs():
        import jax
        import jax.numpy as jnp
        _rk = jax.random.key(seed)
        x = -0.000520686 + 1.00062 * jax.random.normal(jax.random.fold_in(_rk, 1), (16, 32, 750), jnp.float32)
        return x
    x = _rec_inputs()

    def _L0_tok_setup():
        import jax, jax.numpy as jnp
        import numpy as np
        ALPHA = 0.1

        def ewma(y, alpha=ALPHA):
            y_t = jnp.swapaxes(y, 0, 1)

            def step(carry, xt):
                c = alpha * xt + (1.0 - alpha) * carry
                return (c, c)
            _, out = jax.lax.scan(step, y_t[0], y_t[1:])
            out = jnp.concatenate([y_t[:1], out], axis=0)
            return jnp.swapaxes(out, 0, 1)
        key = jax.random.key(seed)
        k1, k2, k3, k4, k5 = jax.random.split(key, 5)
        B, C, T, D = (32, 32, 512, 128)
        x = jax.random.normal(k1, (B, C, T), dtype=jnp.float32)
        W_ve = jax.random.normal(k2, (D, C), dtype=jnp.float32) * (1.0 / np.sqrt(C))
        b_ve = jax.random.normal(k3, (D,), dtype=jnp.float32) * 0.01
        W_lin = jax.random.normal(k4, (D, D), dtype=jnp.float32) * (1.0 / np.sqrt(D))
        b_lin = jax.random.normal(k5, (D,), dtype=jnp.float32) * 0.01
        return {'x': x, 'W_ve': W_ve, 'b_ve': b_ve, 'W_lin': W_lin, 'b_lin': b_lin}
    _L0_tok_all = _L0_tok_setup()
    _L0_tok_in = {k: v for k, v in _L0_tok_all.items() if k in ('W_ve', 'b_ve', 'W_lin', 'b_lin')}
    del _L0_tok_all

    def _L0_attn_setup():
        import jax, jax.numpy as jnp
        import numpy as np
        import math
        HEADS = 8
        key = jax.random.key(seed)
        ks = jax.random.split(key, 9)
        B, T, E = (2, 512, 128)
        s = 1.0 / math.sqrt(E)
        return {'x': jax.random.normal(ks[0], (B, T, E), jnp.float32), 'wq': jax.random.normal(ks[1], (E, E), jnp.float32) * s, 'bq': jax.random.normal(ks[2], (E,), jnp.float32) * s, 'wk': jax.random.normal(ks[3], (E, E), jnp.float32) * s, 'bk': jax.random.normal(ks[4], (E,), jnp.float32) * s, 'wv': jax.random.normal(ks[5], (E, E), jnp.float32) * s, 'bv': jax.random.normal(ks[6], (E,), jnp.float32) * s, 'wg': jax.random.normal(ks[7], (E, E), jnp.float32) * s, 'bg': jax.random.normal(ks[8], (E,), jnp.float32) * s}
    _L0_attn_all = _L0_attn_setup()
    _L0_attn_in = {k: v for k, v in _L0_attn_all.items() if k in ('wq', 'bq', 'wk', 'bk', 'wv', 'bv', 'wg', 'bg')}
    del _L0_attn_all

    def _L0_ffn_setup():
        import jax, jax.numpy as jnp
        import numpy as np
        B, T, D = (4, 2048, 128)
        E, F, CAP = (8, 512, 1024)
        key = jax.random.key(seed)
        ks = jax.random.split(key, 6)
        s = 0.02
        return {'x': jax.random.normal(ks[0], (B, T, D), dtype=jnp.float32), 'Wr': jax.random.normal(ks[1], (D, E), dtype=jnp.float32) * s, 'W1': jax.random.normal(ks[2], (E, D, F), dtype=jnp.float32) * s, 'b1': jax.random.normal(ks[3], (E, F), dtype=jnp.float32) * s, 'W2': jax.random.normal(ks[4], (E, F, D), dtype=jnp.float32) * s, 'b2': jax.random.normal(ks[5], (E, D), dtype=jnp.float32) * s}
    _L0_ffn_all = _L0_ffn_setup()
    _L0_ffn_in = {k: v for k, v in _L0_ffn_all.items() if k in ('Wr', 'W1', 'b1', 'W2', 'b2')}
    del _L0_ffn_all
    return {'x': x, 'L0_tok_W_ve': _L0_tok_in['W_ve'], 'L0_tok_b_ve': _L0_tok_in['b_ve'], 'L0_tok_W_lin': _L0_tok_in['W_lin'], 'L0_tok_b_lin': _L0_tok_in['b_lin'], 'L0_attn_wq': _L0_attn_in['wq'], 'L0_attn_bq': _L0_attn_in['bq'], 'L0_attn_wk': _L0_attn_in['wk'], 'L0_attn_bk': _L0_attn_in['bk'], 'L0_attn_wv': _L0_attn_in['wv'], 'L0_attn_bv': _L0_attn_in['bv'], 'L0_attn_wg': _L0_attn_in['wg'], 'L0_attn_bg': _L0_attn_in['bg'], 'L0_ffn_Wr': _L0_ffn_in['Wr'], 'L0_ffn_W1': _L0_ffn_in['W1'], 'L0_ffn_b1': _L0_ffn_in['b1'], 'L0_ffn_W2': _L0_ffn_in['W2'], 'L0_ffn_b2': _L0_ffn_in['b2']}

def reference(x, L0_tok_W_ve, L0_tok_b_ve, L0_tok_W_lin, L0_tok_b_lin, L0_attn_wq, L0_attn_bq, L0_attn_wk, L0_attn_bk, L0_attn_wv, L0_attn_bv, L0_attn_wg, L0_attn_bg, L0_ffn_Wr, L0_ffn_W1, L0_ffn_b1, L0_ffn_W2, L0_ffn_b2):
    import jax
    import jax.numpy as jnp

    def _L0_tok_ref(x, W_ve, b_ve, W_lin, b_lin):
        import jax, jax.numpy as jnp
        import numpy as np
        ALPHA = 0.1

        def ewma(y, alpha=ALPHA):
            y_t = jnp.swapaxes(y, 0, 1)

            def step(carry, xt):
                c = alpha * xt + (1.0 - alpha) * carry
                return (c, c)
            _, out = jax.lax.scan(step, y_t[0], y_t[1:])
            out = jnp.concatenate([y_t[:1], out], axis=0)
            return jnp.swapaxes(out, 0, 1)
        xt = jnp.transpose(x, (0, 2, 1))
        B, T, C = xt.shape
        x_diff = jnp.concatenate([jnp.zeros((B, 1, C), dtype=xt.dtype), xt[:, 1:, :] - xt[:, :-1, :]], axis=1)
        x_emb = jnp.einsum('btc,dc->btd', x_diff, W_ve) + b_ve
        x_lr = ewma(x_emb)
        x_rl = jnp.flip(ewma(jnp.flip(x_emb, axis=1)), axis=1)
        x_smooth = (x_lr + x_rl) * 0.5
        return jnp.einsum('btd,ed->bte', x_smooth, W_lin) + b_lin

    def _L0_attn_ref(x, wq, bq, wk, bk, wv, bv, wg, bg):
        import jax, jax.numpy as jnp
        import numpy as np
        import math
        HEADS = 8
        B, T, E = x.shape
        H = HEADS
        D = E // H
        gammas = 1.0 - 2.0 ** (-5.0 - jnp.arange(H, dtype=jnp.float32))
        q = (x @ wq.T + bq).reshape(B, T, H, D)
        k = (x @ wk.T + bk).reshape(B, T, H, D)
        v = (x @ wv.T + bv).reshape(B, T, H, D)
        idx = jnp.arange(T)
        rel = idx[None, :] - idx[:, None]
        decay = jnp.where(rel[None] >= 0, gammas[:, None, None] ** rel[None].astype(jnp.float32), 0.0)
        scores = jnp.einsum('bihd,bjhd->bhij', q, k) / math.sqrt(D)
        scores = scores * decay[None]
        out = jnp.einsum('bhij,bjhd->bihd', scores, v).reshape(B, T, E)
        gate = jax.nn.silu(x @ wg.T + bg)
        return gate * out

    def _L0_ffn_ref(x, Wr, W1, b1, W2, b2):
        import jax, jax.numpy as jnp
        import numpy as np
        B, T, D = (4, 2048, 128)
        E, F, CAP = (8, 512, 1024)
        Bb, Tt, Dd = x.shape
        N = Bb * Tt
        C = min(CAP, N)
        x_flat = x.reshape(N, Dd)
        logits = x_flat @ Wr
        probs = jax.nn.softmax(logits, axis=0)
        vals, idx = jax.lax.top_k(probs.T, C)
        selected = x_flat[idx]
        h = jax.nn.gelu(jnp.einsum('ecd,edf->ecf', selected, W1) + b1[:, None, :], approximate=False)
        out_e = jnp.einsum('ecf,efd->ecd', h, W2) + b2[:, None, :]
        weighted = vals[..., None] * out_e
        output = jnp.zeros_like(x_flat).at[idx.reshape(-1)].add(weighted.reshape(-1, Dd))
        return output.reshape(Bb, Tt, Dd)
    h = _L0_tok_ref(x, L0_tok_W_ve, L0_tok_b_ve, L0_tok_W_lin, L0_tok_b_lin)
    h = h + _L0_attn_ref(_layernorm(h, axis=-1), L0_attn_wq, L0_attn_bq, L0_attn_wk, L0_attn_bk, L0_attn_wv, L0_attn_bv, L0_attn_wg, L0_attn_bg)
    h = h + _L0_ffn_ref(_layernorm(h, axis=-1), L0_ffn_Wr, L0_ffn_W1, L0_ffn_b1, L0_ffn_W2, L0_ffn_b2)
    return h

_drawn_inputs = setup_inputs


def setup_inputs(seed=0):
    import zlib

    import numpy as np

    out = dict(_drawn_inputs(seed))
    spreads = {}
    factors = {'L0_ffn_Wr': 64.0,
     'L0_ffn_W1': 64.0,
     'L0_ffn_b1': 200.0,
     'L0_ffn_W2': 64.0,
     'L0_ffn_b2': 200.0}
    for name, (base, spread) in spreads.items():
        noise = np.random.default_rng([zlib.crc32(name.encode()), seed]).standard_normal(out[name].shape)
        drawn = base * np.exp(spread * noise) if base else spread * noise
        out[name] = jnp.asarray(drawn.astype(out[name].dtype))
    for name, factor in factors.items():
        out[name] = (out[name] * factor).astype(out[name].dtype)
    return out
```

```python
from contextlib import ExitStack

import numpy as np

import concourse.bass as bass
from concourse import mybir

F32 = mybir.dt.float32
BF16 = mybir.dt.bfloat16
I32 = mybir.dt.int32
U32 = mybir.dt.uint32
ALU = mybir.AluOpType
ACT = mybir.ActivationFunctionType
AX_X = mybir.AxisListType.X

B, CH, T, D = 16, 32, 750, 128
H, DH = 8, 16
C = 125
NC = T // C
HALF = NC // 2
N = B * T
E, F, CAP = 8, 512, 1024
FT = F // 128
G = CAP // 128
TILES = N // C
ROW = D + E
ALPHA = 0.1
EPS = 1e-5
ROUNDS = 16


class Item:

    def __init__(self, no, pair, slot):
        self.no, self.pair, self.slot = no, pair, slot


def item(no):
    return Item(no, no // 2, no % 2)


UNITS = ["o0", "o1", "h0", "h1", "a5", "a4", "x0", "x1", "a3", "q0", "q1", "k0", "k1", "g0", "g1", "a2",
         "t0", "t1", "v0", "v1", "v2", "a1", "s0", "s1", "b0", "b1", "lg", "a0"]
BANKS = 4
OF_ITEM = {"o": -1, "b": -1, "l": -1, "a": 0}


def bank_of(unit):
    return UNITS.index(unit) % BANKS


def before_in_bank(step, unit):
    at = UNITS.index(unit)
    while True:
        at -= BANKS
        if at < 0:
            at, step = at + len(UNITS), step - 1
        if isinstance(step, int) and step < -1:
            return None, None
        former = UNITS[at]
        no = step + OF_ITEM.get(former[0], 1)
        if not isinstance(no, int) or 0 <= no < B:
            return former, no


def early(it, n):
    return isinstance(it.no, int) and it.no < n


CONSTS = {}


def constants():
    p = np.arange(128)
    head = p // DH
    gamma = 1.0 - 2.0 ** (-5.0 - head.astype(np.float64))
    i = np.arange(C)
    parts = {
        "ident": np.eye(128),
        "keep": (p[:, None] >= i[None, :]),
        "q_decay": gamma[:, None] ** (-i[None, :]) / np.sqrt(DH),
        "k_decay": gamma[:, None] ** i[None, :],
        "chunk_decay": gamma[:, None] ** C,
        "odd_head": (head[:, None] % 2 == 1),
        "block_decay": (head[:, None] == head[None, :]) * gamma[:, None] ** C,
        "same_expert": (p[:, None] % E == p[None, :] % E),
        "earlier_row": (p[:, None] % E == p[None, :] % E) & (p[:, None] // E < p[None, :] // E),
        "expert_of": (p[:, None] % E == np.arange(E)[None, :]),
        "ones": np.ones((128, 128)),
        "steps": np.broadcast_to(0.25 ** np.arange(1, ROUNDS + 2)[None, :], (128, ROUNDS + 1)),
        "k_of": np.broadcast_to(np.arange(1, 4)[None, :], (128, 3)),
        "bound": np.broadcast_to(np.array([N - CAP, N - CAP, N - 2 * CAP])[None, :], (128, 3)),
        "partition": p[:, None],
        "even_odd": np.concatenate([np.broadcast_to(head % 2 == k, (128, 128)) for k in range(2)], axis=1),
        "half": np.full((128, NC), -0.5),
        "numbers": np.broadcast_to(np.concatenate([
            np.arange(128), np.arange(G), (np.arange(B)[None, :] * NC + np.arange(NC)[:, None]).reshape(-1)])[None, :],
            (128, 128 + G + TILES)),
    }
    at = 0
    cols = []
    for name, a in parts.items():
        CONSTS[name] = (at, a.shape[1])
        at += a.shape[1]
        cols.append(a.astype(np.float32))
    return np.ascontiguousarray(np.concatenate(cols, axis=1))


def program(nc, x, w_ve, b_ve, w_lin, b_lin, wq, bq, wk, bk, wv, bv, wg, bg, wr, w1, b1, w2, b2,
            consts, out):
    constants()
    smooth_dram = nc.dram_tensor("smooth_dram", (B, CH, T), F32).ap()
    rows_dram = nc.dram_tensor("rows_dram", (N, ROW), F32).ap()
    out_rows = out.rearrange("b t d -> (b t) d")
    x_rows = x.rearrange("b c t -> (b c) t")
    smooth_rows = smooth_dram.rearrange("b c t -> (b c) t")
    out_items = out.rearrange("b (c p) d -> b p c d", p=C)
    row_items = rows_dram.rearrange("(b c p) d -> b p c d", c=NC, p=C)

    with ExitStack() as ctx:
        def sb(name, shape, dt=F32):
            return ctx.enter_context(nc.sbuf_tensor(name, shape, dt))

        def psum(name, shape, dt=F32):
            return ctx.enter_context(nc.psum_tensor(name, shape, dt))

        def sem(name):
            return ctx.enter_context(nc.semaphore(name))

        cst = sb("cst", [128, consts.shape[1]])
        numbers16 = sb("numbers16", [128, 128 + G + TILES], BF16)

        def const(name, rows=128):
            at, n = CONSTS[name]
            return cst[0:rows, at:at + n]

        ident = const("ident")

        logits = sb("logits", [C, NC, B * E])
        w_col = sb("w_col", [128, 3])
        v_bias_in = sb("v_bias_in", [C, D])
        v_bias = sb("v_bias", [C, 2, D])
        wv_split = sb("wv_split", [D, 2, D])
        wr_sb = sb("wr_sb", [D, E])
        wT = sb("wT", [D, 4, D])
        emb_w = sb("emb_w", [CH + 1, D])
        weight_in = sb("weight_in", [D, 5, D])
        ve_in = sb("ve_in", [D, CH])
        bve_in = sb("bve_in", [D, 1])
        lin_T = sb("lin_T", [D, D])
        blin_in = sb("blin_in", [1, D])

        stage1 = ExitStack()

        def s1(name, shape, dt=F32):
            return stage1.enter_context(nc.sbuf_tensor(name, shape, dt))

        xin = s1("xin", [128, 4, T])
        diff = s1("diff", [128, T])
        scaled = s1("scaled", [128, T])
        fwd = s1("fwd", [128, T])
        bwd = s1("bwd", [128, T])
        smooth = s1("smooth", [128, 4, T])
        keep9 = s1("keep9", [128, T])
        s_in = [s1(f"s_in{k}", [CH + 1, T]) for k in range(2)]
        h_sb = [s1(f"h_sb{k}", [C, NC, D]) for k in range(2)]
        h2_sb = [s1(f"h2_sb{k}", [C, NC, D]) for k in range(2)]
        stats = s1("stats", [C, NC, 6])
        moments = s1("moments", [C, NC, 2])
        rstd = s1("rstd", [C, NC])
        xn = s1("xn", [C, NC, D])
        xT = [s1(f"xT{k}", [D, T]) for k in range(2)]
        q_dec = [s1(f"q_dec{k}", [D, T]) for k in range(2)]
        q_odd = [s1(f"q_odd{k}", [D, T]) for k in range(2)]
        k_dec = [s1(f"k_dec{k}", [D, T]) for k in range(2)]
        k_tok = [s1(f"k_tok{k}", [C, NC, D]) for k in range(2)]
        v_split = [s1(f"v_split{k}", [C, NC, 2, D]) for k in range(2)]
        v_tok = [s1(f"v_tok{k}", [C, NC, D]) for k in range(2)]
        gate = [s1(f"gate{k}", [D, T]) for k in range(2)]
        prob = [s1(f"prob{k}", [C, H, C]) for k in range(2)]
        attn = s1("attn", [D, T])
        state = [s1(f"state{k}", [D, NC - 1, D]) for k in range(2)]
        stats2 = s1("stats2", [C, NC, 6])
        moments2 = s1("moments2", [C, NC, 2])
        rstd2 = s1("rstd2", [C, NC])
        row_sb = [s1(f"row_sb{k}", [C, NC, ROW]) for k in range(2)]
        x2T = s1("x2T", [D, T])

        def p1(name, shape):
            return stage1.enter_context(nc.psum_tensor(name, shape, F32))

        bank = [p1(f"bank{k}", [128, 512]) for k in range(BANKS)]
        ps_score = p1("ps_score", [128, 4, 512])

        consts_in = sem("consts_in")
        x_in = [sem(f"x_in{k}") for k in range(4)]
        scan_step = sem("scan_step")
        smooth_done = sem("smooth_done")
        smooth_out = sem("smooth_out")
        setup_pe = sem("setup_pe")
        setup_act = sem("setup_act")
        ones_set = sem("ones_set")
        s_loaded = [sem(f"s_loaded{k}") for k in range(2)]
        filled = {u: sem(f"filled_{u}") for u in UNITS}
        read = {u: sem(f"read_{u}") for u in UNITS}
        stats_done = sem("stats_done")
        moments_step = sem("moments_step")
        rstd_done = sem("rstd_done")
        xn_done = sem("xn_done")
        q_odd_done = sem("q_odd_done")
        low_scored = sem("low_scored")
        high_scored = sem("high_scored")
        low_masked = sem("low_masked")
        high_copied = sem("high_copied")
        high_masked = sem("high_masked")
        state_step = sem("state_step")
        state_done = sem("state_done")
        stats2_done = sem("stats2_done")
        moments2_step = sem("moments2_step")
        rstd2_done = sem("rstd2_done")
        xn2_done = sem("xn2_done")
        logits_done = sem("logits_done")
        split_done = sem("split_done")
        v_tok_done = sem("v_tok_done")
        h2_out = [sem(f"h2_out{k}") for k in range(2)]
        rows_out = [sem(f"rows_out{k}") for k in range(2)]
        stage1_block = nc.Block()
        stage1.enter_context(stage1_block)
        block = stage1_block

        def chunk(c):
            return slice(c * C, (c + 1) * C)

        def items_of_loop(i, odd):
            if odd:
                return Item(i * 2 + 1, i, 1), Item(i * 2 + 2, i + 1, 0), Item(i * 2 + 3, i + 1, 1)
            return Item(i * 2, i, 0), Item(i * 2 + 1, i, 1), Item(i * 2 + 2, i + 1, 0)

        def all_steps(eng, step):
            step(None, None, item(0))
            step(None, item(0), item(1))
            step(item(0), item(1), item(2))
            step(item(1), item(2), item(3))
            with eng.Fori(1, (B - 2) // 2) as i:
                for odd in range(2):
                    step(*items_of_loop(i, odd))
            step(item(B - 2), item(B - 1), None)
            step(item(B - 1), None, None)

        def prob_free(eng, own, c):
            if c < NC - 2:
                eng.wait_ge(filled[f"a{c + 2}"], own.no + 1)
            elif not early(own, 1):
                eng.wait_ge(filled[f"a{c + 2 - NC}"], own.no)

        def step_no(before, own, after):
            return own.no if own else (after.no - 1 if after else before.no + 1)

        @block.sync
        def _(sp):
            sp.dma_start(cst[:, :], consts).then_inc(consts_in, 16)
            for k, (dst, src) in enumerate([
                    (weight_in[:, 4, :], w_lin), (ve_in[:, :], w_ve), (bve_in[:, :], b_ve.unsqueeze(1)),
                    (blin_in[:, :], b_lin.unsqueeze(0)),
                    (weight_in[:, 0, :], wq), (weight_in[:, 1, :], wk), (weight_in[:, 2, :], wv),
                    (weight_in[:, 3, :], wg), (w_col[:, 0:1], bq.unsqueeze(1)), (w_col[:, 1:2], bk.unsqueeze(1)),
                    (v_bias_in[:, :], bv.unsqueeze(0).broadcast_to([C, D])),
                    (w_col[:, 2:3], bg.unsqueeze(1)),
                    (wr_sb[:, :], wr)]):
                sp.dma_start(dst, src).then_inc(consts_in, 16)
            for j in range(4):
                sp.wait_ge(smooth_done, j + 1)
                sp.dma_start(smooth_rows[j * 128:(j + 1) * 128, :], smooth[:, j, :]).then_inc(smooth_out, 16)
            sp.wait_ge(smooth_out, 64)

            def step(before, own, after):
                if after:
                    if not early(after, 2):
                        sp.wait_ge(filled["h1"], after.no - 1)
                    sp.dma_start(s_in[after.slot][0:CH, :],
                                 smooth_dram[bass.ds(after.no, 1)].rearrange("a c t -> (a c) t")
                                 ).then_inc(s_loaded[after.slot], 16)
                if before:
                    sp.wait_ge(read["o1"], before.no + 1)
                    sp.dma_start(out_items[bass.ds(before.no, 1)].rearrange("a p c d -> (a p) c d"),
                                 h2_sb[before.slot][:, :, :]).then_inc(h2_out[before.slot], 16)
                    sp.wait_ge(xn2_done, before.no + 1)
                    sp.wait_ge(logits_done, before.no + 1)
                    sp.dma_start(row_items[bass.ds(before.no, 1)].rearrange("a p c d -> (a p) c d"),
                                 row_sb[before.slot][:, :, :]).then_inc(rows_out[before.slot], 16)

            all_steps(sp, step)
            for k in range(2):
                sp.wait_ge(h2_out[k], 16 * B // 2)
                sp.wait_ge(rows_out[k], 16 * B // 2)

        @block.tensor
        def _(pe):
            pe.wait_ge(consts_in, 16 * 14)
            pe.transpose(bank[0][:, 0:D], weight_in[:, 4, :], ident).then_inc(setup_pe, 1)
            for k in range(4):
                t = pe.transpose(bank[1][:, k * D:(k + 1) * D], weight_in[:, k, :], ident)
            t.then_inc(setup_pe, 1)
            pe.wait_ge(setup_act, 1)
            pe.matmul(bank[2][0:CH, 0:D], ve_in[:, :], lin_T[:, :], start=True, stop=True)
            pe.matmul(bank[2][CH:CH + 1, D:2 * D], bve_in[:, :], lin_T[:, :], start=True, stop=False,
                      skip_group_check=True)
            pe.matmul(bank[2][CH:CH + 1, D:2 * D], const("ones")[0:1, 0:1], blin_in[:, :], start=False, stop=True,
                      skip_group_check=True).then_inc(setup_pe, 1)
            pe.wait_ge(setup_act, 4)
            pe.wait_ge(split_done, 1)

            def claim(step, unit):
                former, no = before_in_bank(step, unit)
                if former:
                    pe.wait_ge(read[former], no + 1)
                return bank[bank_of(unit)]

            def scores(own, c):
                done = own.no * NC + (NC - 1 - c)
                if c == NC - 1:
                    pe.wait_ge(read["q1"], own.no + 1)
                    pe.wait_ge(q_odd_done, own.no + 1)
                    pe.wait_ge(read["k1"], own.no + 1)
                pe.wait_ge(low_masked, done)
                pe.wait_ge(high_copied, done)
                for h in (0, 2, 4, 6, 1, 3, 5, 7):
                    g, lo = h // 2, 32 * (h // 2)
                    rows = slice(lo, lo + 32) if h % 2 else slice(lo, lo + DH)
                    q = (q_odd if h % 2 else q_dec)[own.slot]
                    at = (h % 2) * C
                    m = pe.matmul(ps_score[0:C, g, at:at + C], k_dec[own.slot][rows, chunk(c)], q[rows, chunk(c)],
                                  start=True, stop=True)
                    if h == 3:
                        m.then_inc(low_scored, 1)
                m.then_inc(high_scored, 1)

            def values(own, c):
                unit = f"a{c}"
                o = claim(own.no, unit)[:, 0:C]
                if c == NC - 1:
                    pe.wait_ge(state_done, own.no + 1)
                else:
                    pe.matmul(o, state[own.slot][:, c, :], q_dec[own.slot][:, chunk(c)], start=True, stop=False,
                              skip_group_check=True)
                pe.wait_ge(low_masked, own.no * NC + (NC - c))
                pe.wait_ge(high_masked, own.no * NC + (NC - c))
                for k, h in enumerate((0, 2, 4, 6, 1, 3, 5, 7)):
                    rows = slice(h // 2 * 32, h // 2 * 32 + 32)
                    m = pe.matmul(o[rows, :], v_split[own.slot][:, c, h % 2, rows], prob[c % 2][:, h, :],
                                  start=(c == NC - 1 and k < 4), stop=(k >= 4), skip_group_check=True)
                m.then_inc(filled[unit], 1)

            def step(before, own, after):
                n = step_no(before, own, after)

                def h_units():
                    if early(after, 1):
                        pe.wait_ge(ones_set, 1)
                    pe.wait_ge(s_loaded[after.slot], after.pair * 16 + 16)
                    for k in range(2):
                        ps = claim(n, f"h{k}")
                        for c in range(HALF):
                            m = pe.matmul(ps[0:C, c * D:(c + 1) * D], s_in[after.slot][:, chunk(k * HALF + c)],
                                          emb_w[:, :], start=True, stop=True)
                        m.then_inc(filled[f"h{k}"], 1)

                def x_units():
                    pe.wait_ge(xn_done, after.no + 1)
                    for k in range(2):
                        ps = claim(n, f"x{k}")
                        for c in range(HALF):
                            m = pe.transpose(ps[:, chunk(c)], xn[:, k * HALF + c, :], ident[0:C, 0:C])
                        m.then_inc(filled[f"x{k}"], 1)

                def o_units():
                    for k in range(2):
                        pe.wait_ge(read["a0"], before.no + 1)
                        ps = claim(n, f"o{k}")
                        for c in range(HALF):
                            m = pe.transpose(ps[0:C, c * D:(c + 1) * D], attn[:, chunk(k * HALF + c)], ident)
                        m.then_inc(filled[f"o{k}"], 1)

                def project(name, w):
                    for k in range(2):
                        ps = claim(n, f"{name}{k}")
                        pe.wait_ge(read[f"x{k}"], after.no + 1)
                        pe.matmul(ps[:, 0:HALF * C], wT[:, w, :], xT[after.slot][:, k * HALF * C:(k + 1) * HALF * C],
                                  start=True, stop=True).then_inc(filled[f"{name}{k}"], 1)

                def k_tok_units():
                    for k in range(2):
                        pe.wait_ge(read[f"k{k}"], after.no + 1)
                        ps = claim(n, f"t{k}")
                        for c in range(HALF):
                            m = pe.transpose(ps[0:C, c * D:(c + 1) * D], k_dec[after.slot][:, chunk(k * HALF + c)],
                                             ident)
                        m.then_inc(filled[f"t{k}"], 1)

                def v_units():
                    for k in range(3):
                        ps = claim(n, f"v{k}")
                        for c in range(2):
                            m = pe.matmul(ps[0:C, c * 2 * D:(c + 1) * 2 * D], xT[after.slot][:, chunk(2 * k + c)],
                                          wv_split[:, :, :], start=True, stop=True)
                        m.then_inc(filled[f"v{k}"], 1)

                def state_units():
                    pe.wait_ge(read["t1"], after.no + 1)
                    pe.wait_ge(v_tok_done, after.no + 1)
                    for k, cs in enumerate(([4, 3, 2, 1], [0])):
                        ps = claim(n, f"s{k}")
                        for c in cs:
                            at = (c - cs[-1]) * D
                            m = pe.matmul(ps[:, at:at + D], k_tok[after.slot][:, c + 1, :],
                                          v_tok[after.slot][:, c + 1, :], start=True, stop=True)
                        m.then_inc(filled[f"s{k}"], 1)

                def back():
                    pe.wait_ge(xn2_done, before.no + 1)
                    for k in range(2):
                        ps = claim(n, f"b{k}")
                        for c in range(HALF):
                            m = pe.transpose(ps[:, chunk(c)], row_sb[before.slot][:, k * HALF + c, 0:D],
                                             ident[0:C, 0:C])
                        m.then_inc(filled[f"b{k}"], 1)
                    pe.wait_ge(read["b1"], before.no + 1)
                    ps = claim(n, "lg")
                    for c in range(NC):
                        m = pe.matmul(ps[0:C, c * E:(c + 1) * E], x2T[:, chunk(c)], wr_sb[:, :], start=True, stop=True)
                    m.then_inc(filled["lg"], 1)

                if own:
                    scores(own, 5)
                if before:
                    o_units()
                if after:
                    h_units()
                if own:
                    values(own, 5)
                    scores(own, 4)
                    values(own, 4)
                    scores(own, 3)
                if after:
                    x_units()
                if own:
                    values(own, 3)
                    scores(own, 2)
                if after:
                    project("q", 0)
                    project("k", 1)
                    project("g", 3)
                if own:
                    values(own, 2)
                    scores(own, 1)
                if after:
                    k_tok_units()
                    v_units()
                if own:
                    values(own, 1)
                    scores(own, 0)
                if after:
                    state_units()
                if before:
                    back()
                if own:
                    values(own, 0)

            all_steps(pe, step)

        @block.scalar
        def _(act):
            act.dma_start(xin[:, 0, :], x_rows[0:128, :]).then_inc(x_in[0], 16)
            for j in range(1, 4):
                act.dma_start(xin[:, j, :], x_rows[j * 128:(j + 1) * 128, :]).then_inc(x_in[j], 16)
            act.wait_ge(setup_pe, 1)
            act.copy(lin_T[:, :], bank[0][:, 0:D]).then_inc(setup_act, 1)
            act.wait_ge(setup_pe, 2)
            act.copy(wT[:, :, :].rearrange("p k d -> p (k d)"), bank[1][:, :]).then_inc(setup_act, 1)
            act.wait_ge(setup_pe, 3)
            act.copy(emb_w[0:CH, :], bank[2][0:CH, 0:D]).then_inc(setup_act, 1)
            act.copy(emb_w[CH:CH + 1, :], bank[2][CH:CH + 1, D:2 * D]).then_inc(setup_act, 1)

            def step(before, own, after):
                n = step_no(before, own, after)

                def copy_out(it, unit, dst, rows, cols):
                    act.wait_ge(filled[unit], it.no + 1)
                    act.copy(dst, bank[bank_of(unit)][0:rows, 0:cols]).then_inc(read[unit], 1)

                def high_scores(c):
                    act.wait_ge(high_scored, own.no * NC + (NC - c))
                    prob_free(act, own, c)
                    act.copy(prob[c % 2][:, H // 2:H, :].rearrange("p (g e) i -> p g (e i)", e=2),
                             ps_score[0:C, 2:4, 0:2 * C]).then_inc(high_copied, 1)

                if own:
                    high_scores(5)
                if after:
                    if not early(after, 2):
                        act.wait_ge(read["o1"], after.no - 1)
                    for k in range(2):
                        copy_out(after, f"h{k}", h_sb[after.slot][:, k * HALF:(k + 1) * HALF, :].rearrange("p c d -> p (c d)"),
                                 C, HALF * D)
                if own:
                    high_scores(4)
                    high_scores(3)
                if after:
                    if not early(after, 2):
                        act.wait_ge(filled["v2"], after.no - 1)
                    for k in range(2):
                        copy_out(after, f"x{k}", xT[after.slot][:, k * HALF * C:(k + 1) * HALF * C], D, HALF * C)
                if own:
                    high_scores(2)
                if after:
                    if not early(after, 2):
                        act.wait_ge(read["a0"], after.no - 1)
                    for k in range(2):
                        act.wait_ge(filled[f"g{k}"], after.no + 1)
                        act.activation(gate[after.slot][:, k * HALF * C:(k + 1) * HALF * C],
                                       bank[bank_of(f"g{k}")][:, 0:HALF * C], ACT.Silu,
                                       bias=w_col[:, 2:3]).then_inc(read[f"g{k}"], 1)
                if own:
                    high_scores(1)
                if after:
                    for k in range(2):
                        copy_out(after, f"t{k}", k_tok[after.slot][:, k * HALF:(k + 1) * HALF, :].rearrange("p c d -> p (c d)"),
                                 C, HALF * D)
                if own:
                    high_scores(0)
                if before:
                    if not early(before, 1):
                        act.wait_ge(filled["lg"], before.no)
                    for k in range(2):
                        copy_out(before, f"b{k}", x2T[:, k * HALF * C:(k + 1) * HALF * C], D, HALF * C)

            all_steps(act, step)

        @block.gpsimd
        def _(pool):
            pool.memset(s_in[0][CH:CH + 1, :], 1.0)
            pool.memset(s_in[1][CH:CH + 1, :], 1.0).then_inc(ones_set, 1)
            pool.wait_ge(consts_in, 16 * 14)

            def step(before, own, after):
                def high_mask(c):
                    done = own.no * NC + (NC - 1 - c)
                    pool.wait_ge(high_copied, done + 1)
                    p = prob[c % 2][:, H // 2:H, :]
                    pool.tensor_tensor(p, p, const("keep", C).unsqueeze(1).broadcast_to([C, H // 2, C]),
                                       ALU.mult).then_inc(high_masked, 1)

                def inverse_root(moments_ready, done, m, r):
                    pool.wait_ge(moments_ready, done)
                    return pool.tensor_tensor(r[:, :], m[:, :, 1], const("half", C), ALU.pow)

                if own:
                    high_mask(5)
                if after:
                    inverse_root(moments_step, 2 * after.no + 2, moments, rstd).then_inc(rstd_done, 1)
                if own:
                    high_mask(4)
                if before:
                    inverse_root(moments2_step, 2 * before.no + 2, moments2, rstd2).then_inc(rstd2_done, 1)
                if own:
                    high_mask(3)
                    high_mask(2)
                if after:
                    pool.wait_ge(read["q0"], after.no + 1)
                    pool.wait_ge(read["q1"], after.no + 1)
                    pool.tensor_tensor(q_odd[after.slot][:, :], q_dec[after.slot][:, :],
                                       const("odd_head").broadcast_to([D, T]), ALU.mult).then_inc(q_odd_done, 1)
                if own:
                    high_mask(1)
                if after:
                    pool.wait_ge(read["v2"], after.no + 1)
                    pool.tensor_tensor(v_tok[after.slot][:, :, :], v_split[after.slot][:, :, 0, :],
                                       v_split[after.slot][:, :, 1, :], ALU.add).then_inc(v_tok_done, 1)
                if own:
                    high_mask(0)

            all_steps(pool, step)

        @block.vector
        def _(dve):
            dve.memset(keep9[:, :], 1.0 - ALPHA)
            dve.memset(diff[:, 0:1], 0.0).then_inc(scan_step, 1)
            for j in range(4):
                dve.wait_ge(x_in[j], 16)
                if j:
                    dve.wait_ge(smooth_done, j)
                dve.tensor_tensor(diff[:, 1:T], xin[:, j, 1:T], xin[:, j, 0:T - 1], ALU.subtract).then_inc(scan_step, 1)
                dve.wait_ge(scan_step, 5 * j + 2)
                dve.tensor_scalar(scaled[:, :], diff[:, :], 0.5 * ALPHA, None, ALU.mult).then_inc(scan_step, 1)
                dve.wait_ge(scan_step, 5 * j + 3)
                dve.tensor_tensor_scan(fwd[:, :], keep9[:, :], scaled[:, :], 0.0, ALU.mult, ALU.add).then_inc(scan_step, 1)
                dve.wait_ge(scan_step, 5 * j + 4)
                dve.tensor_scalar(scaled[:, T - 1:T], diff[:, T - 1:T], 0.5, None, ALU.mult).then_inc(scan_step, 1)
                dve.wait_ge(scan_step, 5 * j + 5)
                dve.tensor_tensor_scan(bwd[:, ::-1], keep9[:, :], scaled[:, ::-1], 0.0, ALU.mult,
                                       ALU.add).then_inc(scan_step, 1)
                dve.wait_ge(scan_step, 5 * j + 6)
                dve.tensor_tensor(smooth[:, j, :], fwd[:, :], bwd[:, :], ALU.add).then_inc(smooth_done, 1)
            dve.wait_ge(consts_in, 16 * 14)
            dve.wait_ge(setup_act, 2)
            halves = const("even_odd").rearrange("p (k d) -> p k d", k=2)
            dve.tensor_tensor(wv_split[:, :, :], wT[:, 2:3, :].broadcast_to([D, 2, D]), halves, ALU.mult)
            dve.tensor_tensor(v_bias[:, :, :], v_bias_in[:, :].unsqueeze(1).broadcast_to([C, 2, D]), halves[0:C],
                              ALU.mult).then_inc(split_done, 1)
            dve.wait_ge(split_done, 1)

            def step(before, own, after):
                n = step_no(before, own, after)

                def low_scores(c):
                    dve.wait_ge(low_scored, own.no * NC + (NC - c))
                    prob_free(dve, own, c)
                    keep = const("keep", C).unsqueeze(1).unsqueeze(1).broadcast_to([C, 2, 2, C])
                    dve.tensor_tensor(prob[c % 2][:, 0:H // 2, :].rearrange("p (g e) i -> p g e i", e=2),
                                      ps_score[0:C, 0:2, 0:2 * C].rearrange("p g (e i) -> p g e i", e=2),
                                      keep, ALU.mult).then_inc(low_masked, 1)

                def states():
                    st = state[after.slot]
                    for k, (lo, hi) in enumerate(((1, NC - 1), (0, 1))):
                        dve.wait_ge(filled[f"s{k}"], after.no + 1)
                        dve.tensor_tensor(st[:, lo:hi, :],
                                          bank[bank_of(f"s{k}")][:, 0:(hi - lo) * D].rearrange("p (c d) -> p c d", d=D),
                                          const("block_decay").unsqueeze(1).broadcast_to([D, hi - lo, D]),
                                          ALU.mult).then_inc(read[f"s{k}"], 1)
                    dve.wait_ge(read["s1"], after.no + 1)
                    for k, c in enumerate(range(NC - 3, -1, -1)):
                        if k:
                            dve.wait_ge(state_step, after.no * (NC - 3) + k)
                        i = dve.scalar_tensor_tensor(st[:, c, :], st[:, c + 1, :], const("chunk_decay"), st[:, c, :],
                                                     ALU.mult, ALU.add)
                        i.then_inc(state_done if c == 0 else state_step, 1)

                def gated_out(c):
                    if c == NC - 1:
                        dve.wait_ge(read["g1"], own.no + 1)
                        if not early(own, 1):
                            dve.wait_ge(filled["o1"], own.no)
                    dve.wait_ge(filled[f"a{c}"], own.no + 1)
                    dve.tensor_tensor(attn[:, chunk(c)], bank[bank_of(f"a{c}")][:, 0:C], gate[own.slot][:, chunk(c)],
                                      ALU.mult).then_inc(read[f"a{c}"], 1)

                def residual():
                    if not early(before, 2):
                        dve.wait_ge(h2_out[before.slot], before.pair * 16)
                    for k in range(2):
                        cs = slice(k * HALF, (k + 1) * HALF)
                        dve.wait_ge(filled[f"o{k}"], before.no + 1)
                        dve.tensor_tensor(h2_sb[before.slot][:, cs, :],
                                          bank[bank_of(f"o{k}")][0:C, 0:HALF * D].rearrange("p (c d) -> p c d", d=D),
                                          h_sb[before.slot][:, cs, :], ALU.add).then_inc(read[f"o{k}"], 1)

                def norm_stats(src, st, st_done, mo, mo_step, no):
                    for c in range(NC):
                        i = dve.bn_stats(st[:, c, :], src[:, c, :])
                    i.then_inc(st_done, 1)
                    dve.wait_ge(consts_in, 16 * 14)
                    dve.wait_ge(st_done, no + 1)
                    for c in range(NC):
                        i = dve.bn_aggr(mo[:, c, :], st[:, c, :])
                    i.then_inc(mo_step, 1)
                    dve.wait_ge(mo_step, 2 * no + 1)
                    dve.tensor_scalar(mo[:, :, 1], mo[:, :, 1], EPS, None, ALU.add).then_inc(mo_step, 1)

                def normalise(dst, src, mo, r, r_done, done, no):
                    dve.wait_ge(r_done, no + 1)
                    for c in range(NC):
                        i = dve.tensor_scalar(dst[:, c, 0:D], src[:, c, :], mo[:, c, 0:1], r[:, c:c + 1],
                                              ALU.subtract, ALU.mult)
                    i.then_inc(done, 1)

                def projected(unit, k, dst, bias, decay):
                    b = bank_of(unit)
                    dve.wait_ge(filled[unit], after.no + 1)
                    cols = slice(k * HALF * C, (k + 1) * HALF * C)
                    dve.scalar_tensor_tensor(
                        dst[:, cols].rearrange("p (c i) -> p c i", i=C),
                        bank[b][:, 0:HALF * C].rearrange("p (c i) -> p c i", i=C), bias,
                        decay.unsqueeze(1).broadcast_to([128, HALF, C]), ALU.add, ALU.mult).then_inc(read[unit], 1)

                if own:
                    low_scores(5)
                if before:
                    residual()
                if after:
                    dve.wait_ge(read["h1"], after.no + 1)
                    norm_stats(h_sb[after.slot], stats, stats_done, moments, moments_step, after.no)
                if own:
                    gated_out(5)
                    low_scores(4)
                if before:
                    dve.wait_ge(read["o1"], before.no + 1)
                    norm_stats(h2_sb[before.slot], stats2, stats2_done, moments2, moments2_step, before.no)
                if own:
                    gated_out(4)
                    low_scores(3)
                if after:
                    if not early(after, 1):
                        dve.wait_ge(filled["x1"], after.no)
                    normalise(xn, h_sb[after.slot], moments, rstd, rstd_done, xn_done, after.no)
                if own:
                    gated_out(3)
                    low_scores(2)
                if before:
                    if not early(before, 2):
                        dve.wait_ge(rows_out[before.slot], before.pair * 16)
                    normalise(row_sb[before.slot], h2_sb[before.slot], moments2, rstd2, rstd2_done, xn2_done,
                              before.no)
                if after:
                    if not early(after, 2):
                        dve.wait_ge(filled["a0"], after.no - 1)
                    for k in range(2):
                        projected(f"q{k}", k, q_dec[after.slot], w_col[:, 0:1], const("q_decay"))
                    for k in range(2):
                        projected(f"k{k}", k, k_dec[after.slot], w_col[:, 1:2], const("k_decay"))
                if own:
                    gated_out(2)
                    low_scores(1)
                if after:
                    for k in range(3):
                        dve.wait_ge(filled[f"v{k}"], after.no + 1)
                        dve.tensor_tensor(v_split[after.slot][:, 2 * k:2 * k + 2, :, :],
                                          bank[bank_of(f"v{k}")][0:C, :].rearrange("p (c w d) -> p c w d", c=2, w=2),
                                          v_bias[:, :, :].unsqueeze(1).broadcast_to([C, 2, 2, D]),
                                          ALU.add).then_inc(read[f"v{k}"], 1)
                if own:
                    gated_out(1)
                    low_scores(0)
                if after:
                    states()
                if before:
                    dve.wait_ge(filled["lg"], before.no + 1)
                    lg = bank[bank_of("lg")][0:C, 0:NC * E].rearrange("p (c e) -> p c e", e=E)
                    dve.tensor_copy(row_sb[before.slot][:, :, D:ROW], lg).then_inc(logits_done, 1)
                    dve.tensor_copy(logits[:, :, bass.ds(before.no * E, E)], lg).then_inc(read["lg"], 1)
                if own:
                    gated_out(0)

            all_steps(dve, step)
        stage1.close()

        def s2(name, shape, dt=F32):
            return ctx.enter_context(nc.sbuf_tensor(name, shape, dt))

        lg_rows = s2("lg_rows", [128, T])
        scratch = s2("scratch", [128, T])
        scratch_act = s2("scratch_act", [128, T])
        row_ends = s2("row_ends", [128, 2])
        ends = s2("ends", [1, 2, E])
        ends_all = s2("ends_all", [128, 2, E])
        ends_sel = s2("ends_sel", [128, 2, E])
        top_low = s2("top_low", [128, 2])
        neg_top = s2("neg_top", [128, 1 + E])
        exp_sum = s2("exp_sum", [128, 1])
        exp_sums = s2("exp_sums", [128, E])
        inv_sum = s2("inv_sum", [128, E])
        low = s2("low", [128, 1])
        width = s2("width", [128, 1])
        thresholds = s2("thresholds", [128, 3])
        counts = s2("counts", [128, 3])
        passed = s2("passed", [128, 3])
        n_passed = s2("n_passed", [128, 1])
        high = s2("high", [128, 1])
        sure = s2("sure", [128, T])
        band = s2("band", [128, T])
        row_counts = s2("row_counts", [128, 2])
        offsets = s2("offsets", [128, 3])
        sure_rank = s2("sure_rank", [128, T])
        band_rank = s2("band_rank", [128, T])
        place = s2("place", [128, T])
        place_tok = s2("place_tok", [C, E, TILES], I32)
        place_int = s2("place_int", [C, E, TILES], I32)
        block16 = s2("block16", [C, E, TILES], BF16)
        slot16 = s2("slot16", [C, E, TILES], BF16)
        slot_hot = [s2(f"slot_hot{k}", [C, TILES, 128], BF16) for k in range(2)]
        block_hot = s2("block_hot", [C, TILES, G], BF16)
        block_val = [s2(f"block_val{k}", [C, TILES, 2 * G], BF16) for k in range(2)]
        carrier = s2("carrier", [1, 1])
        idx_tile = s2("idx_tile", [128, G])
        idx = [s2(f"idx{k}", [128, G], U32) for k in range(2)]
        taken = [s2(f"taken{k}", [128, G, ROW]) for k in range(2)]
        takenT = s2("takenT", [D, CAP])
        hidden = s2("hidden", [128, FT, CAP])
        weight_exp = s2("weight_exp", [128, G])
        weight = s2("weight", [128, G])
        y_sum = s2("y_sum", [128, G, D])
        y = [s2(f"y{k}", [128, G, D]) for k in range(2)]
        w1_sb = [s2(f"w1_sb{k}", [D, F]) for k in range(2)]
        w2_sb = [s2(f"w2_sb{k}", [128, FT, D]) for k in range(2)]
        b1_sb = [s2(f"b1_sb{k}", [128, FT]) for k in range(2)]
        b2_sb = [s2(f"b2_sb{k}", [128, D]) for k in range(2)]

        banks = [psum(f"bank2_{k}", [128, 512]) for k in range(8)]
        ps_idx, ps_T, ps_H, ps_Y = banks[0], banks[1:3], banks[3:6], banks[6:8]

        turned = sem("turned")
        lg_copied = sem("lg_copied")
        dve_step = sem("dve_step")
        ends_turned = sem("ends_turned")
        ends_done = sem("ends_done")
        ends_spread = sem("ends_spread")
        top_done = sem("top_done")
        exp_done = sem("exp_done")
        exp_sums_done = sem("exp_sums_done")
        sums_spread = sem("sums_spread")
        thresholds_set = sem("thresholds_set")
        counted_dve = sem("counted_dve")
        counted_act = sem("counted_act")
        totals_done = sem("totals_done")
        round_step = sem("round_step")
        rows_counted = sem("rows_counted")
        offsets_done = sem("offsets_done")
        place_done = sem("place_done")
        place_turned = sem("place_turned")
        split_step = sem("split_step")
        hot_step = sem("hot_step")
        hot_done = sem("hot_done")
        idx_ps = sem("idx_ps")
        idx_step = sem("idx_step")
        carried = sem("carried")
        idx_done = sem("idx_done")
        taken_in = [sem(f"taken_in{k}") for k in range(2)]
        taken_turned = sem("taken_turned")
        takenT_done = sem("takenT_done")
        hidden_ps = sem("hidden_ps")
        hidden_done = sem("hidden_done")
        weight_step = sem("weight_step")
        weight_done = sem("weight_done")
        y_ps = sem("y_ps")
        y_step = sem("y_step")
        y_done = sem("y_done")
        added = [sem(f"added{k}") for k in range(2)]
        weights_in = [sem(f"weights_in{k}") for k in range(2)]

        block = ctx.enter_context(nc.Block())

        def all_experts(eng, step):
            step(item(0), False)
            step(item(1), False)
            with eng.Fori(1, E // 2 - 1) as i:
                step(Item(i * 2, i, 0), False)
                step(Item(i * 2 + 1, i, 1), False)
            step(item(E - 2), True)
            step(item(E - 1), True)

        @block.sync
        def _(sp):
            def load(it):
                if not early(it, 2):
                    sp.wait_ge(y_done, 2 * (it.no - 1))
                for dst, src in ((w1_sb, w1), (w2_sb, w2), (b1_sb, b1), (b2_sb, b2)):
                    a = src[bass.ds(it.no, 1)]
                    if src is w1:
                        a = a.rearrange("a d f -> (a d) f")
                    elif src is w2:
                        a = a.rearrange("a (p t) d -> (a p) t d", t=FT)
                    elif src is b1:
                        a = a.rearrange("a (p t) -> (a p) t", t=FT)
                    else:
                        a = a.broadcast_to([128, D])
                    sp.dma_start(dst[it.slot][tuple(slice(None) for _ in a.shape)], a).then_inc(weights_in[it.slot], 16)

            load(item(0))
            load(item(1))
            with sp.Fori(1, E // 2) as i:
                load(Item(i * 2, i, 0))
                load(Item(i * 2 + 1, i, 1))

        @block.tensor
        def _(pe):
            for c in range(NC):
                m = pe.transpose(banks[c // HALF][:, chunk(c % HALF)], logits[:, c, :], ident[0:C, 0:C])
                if c % HALF == HALF - 1:
                    m.then_inc(turned, 1)
            pe.wait_ge(dve_step, 2)
            for k in range(2):
                m = pe.transpose(banks[2][0:1, k * 128:(k + 1) * 128], row_ends[:, k:k + 1], ident)
            m.then_inc(ends_turned, 1)
            pe.wait_ge(ends_done, 2)
            pe.matmul(banks[3][:, 0:2 * E], const("ones")[0:1, :], ends[:, :, :].rearrange("p k e -> p (k e)"),
                      start=True, stop=True).then_inc(ends_spread, 1)
            pe.wait_ge(exp_sums_done, 1)
            pe.matmul(banks[4][:, 0:E], const("ones"), exp_sums[:, :], start=True, stop=True).then_inc(sums_spread, 1)
            with pe.Fori(0, ROUNDS) as r:
                pe.wait_ge(counted_dve, r * 2 + 2)
                pe.wait_ge(counted_act, r + 1)
                pe.matmul(banks[5][:, 0:3], const("same_expert"), counts[:, :], start=True,
                          stop=True).then_inc(totals_done, 1)
            pe.wait_ge(rows_counted, 1)
            pe.matmul(banks[6][:, 0:2], const("earlier_row"), row_counts[:, :], start=True, stop=True)
            pe.matmul(banks[6][:, 2:3], const("same_expert"), row_counts[:, 0:1], start=True,
                      stop=True).then_inc(offsets_done, 1)
            pe.wait_ge(place_done, 1)
            for c in range(NC):
                m = pe.transpose(banks[c // 4][0:C, (c % 4) * 128:(c % 4 + 1) * 128], place[:, chunk(c)], ident)
                if c in (3, NC - 1):
                    m.then_inc(place_turned, 1)

            def index(it):
                pe.wait_ge(hot_done, it.no + 1)
                pe.wait_ge(idx_done, it.no)
                for t in range(TILES):
                    m = pe.matmul(ps_idx[:, 0:2 * G], slot_hot[it.slot][:, t, :], block_val[it.slot][:, t, :],
                                  start=(t == 0), stop=(t == TILES - 1))
                m.then_inc(idx_ps, 1)

            pe.wait_ge(split_step, 2)
            index(item(0))

            def step(it, last):
                if not (last and it.slot == 1):
                    index(Item(it.no + 1, it.pair + it.slot, 1 - it.slot))
                pe.wait_ge(taken_in[it.slot], it.pair * 128 + 128)
                for k in range(2):
                    pe.wait_ge(takenT_done, it.no * 2)
                    for g in range(4):
                        m = pe.transpose(ps_T[k][:, g * 128:(g + 1) * 128], taken[it.slot][:, 4 * k + g, 0:D], ident)
                    m.then_inc(taken_turned, 1)
                pe.wait_ge(weights_in[it.slot], it.pair * 64 + 64)
                u = 0
                for k in range(2):
                    pe.wait_ge(takenT_done, it.no * 2 + k + 1)
                    for f in range(FT):
                        if u < 3:
                            pe.wait_ge(hidden_done, it.no * 8)
                        else:
                            pe.wait_ge(hidden_done, it.no * 8 + u - 2)
                        pe.matmul(ps_H[u % 3][:, :], w1_sb[it.slot][:, f * 128:(f + 1) * 128],
                                  takenT[:, k * 512:(k + 1) * 512], start=True, stop=True).then_inc(hidden_ps, 1)
                        u += 1
                for g in range(G):
                    if g % 4 == 0:
                        pe.wait_ge(hidden_done, it.no * 8 + 4 + g)
                        pe.wait_ge(y_done, it.no * 2)
                    for f in range(FT):
                        m = pe.matmul(ps_Y[g // 4][:, (g % 4) * D:(g % 4 + 1) * D],
                                      hidden[:, f, g * 128:(g + 1) * 128], w2_sb[it.slot][:, f, :],
                                      start=(f == 0), stop=(f == FT - 1), skip_group_check=True)
                    if g % 4 == 3:
                        m.then_inc(y_ps, 1)

            all_experts(pe, step)

        @block.scalar
        def _(act):
            act.wait_ge(top_done, 1)
            act.activation(scratch_act[:, :], lg_rows[:, :], ACT.Exp, bias=neg_top[:, 0:1],
                           accum_out=exp_sum[:, :]).then_inc(exp_done, 1)
            act.wait_ge(exp_done, 1)
            with act.Fori(0, ROUNDS) as r:
                act.wait_ge(thresholds_set, r + 1)
                act.activation(scratch_act[:, :], lg_rows[:, :], ACT.Sign, bias=thresholds[:, 2:3], scale=-1.0,
                               accum_out=counts[:, 2:3]).then_inc(counted_act, 1)
                act.wait_ge(counted_act, r + 1)

            def step(it, last):
                act.wait_ge(taken_in[it.slot], it.pair * 128 + 128)
                act.wait_ge(weight_done, it.no)
                act.activation(weight_exp[:, :], taken[it.slot][:, :, bass.ds(it.no + D, 1)].rearrange("p g a -> p (g a)"),
                               ACT.Exp, bias=neg_top[:, bass.ds(it.no + 1, 1)]).then_inc(weight_step, 1)
                for k in range(2):
                    act.wait_ge(taken_turned, it.no * 2 + k + 1)
                    act.wait_ge(hidden_ps, it.no * 8)
                    act.copy(takenT[:, k * 512:(k + 1) * 512], ps_T[k][:, :]).then_inc(takenT_done, 1)
                act.wait_ge(weights_in[it.slot], it.pair * 64 + 64)
                act.wait_ge(y_ps, it.no * 2)
                for u in range(2 * FT):
                    act.wait_ge(hidden_ps, it.no * 8 + u + 1)
                    k, f = u // FT, u % FT
                    act.activation(hidden[:, f, k * 512:(k + 1) * 512], ps_H[u % 3][:, :], ACT.Gelu,
                                   bias=b1_sb[it.slot][:, f:f + 1]).then_inc(hidden_done, 1)

            all_experts(act, step)

        @block.gpsimd
        def _(pool):
            last_token = pool.to_reg(N - 1)

            def carry_waits(count):
                pool.wait_ge(carried, count)
                pool.tensor_tensor(carrier[:, :], const("ones")[0:1, 0:1], const("ones")[0:1, 0:1],
                                   ALU.mult).then_inc(carried, 1)

            def take(it):
                pool.wait_ge(idx_done, it.no + 1)
                if not early(it, 2):
                    pool.wait_ge(taken_turned, it.no * 2 - 2)
                    pool.wait_ge(weight_step, it.no - 1)
                carry_waits(0 if early(it, 1) else it.no * 3 - 2)
                for g in range(G):
                    pool.indirect_dma_start(
                        out=taken[it.slot][:, g, :], out_offset=None, in_=rows_dram[:, :],
                        in_offset=bass.IndirectOffsetOnAxis(ap=idx[it.slot][:, g:g + 1], axis=0),
                        bounds_check=last_token, oob_is_err=False).then_inc(taken_in[it.slot], 16)

            take(item(0))

            def step(it, last):
                if not (last and it.slot == 1):
                    after = Item(it.no + 1, it.pair + it.slot, 1 - it.slot)
                    take(after)
                for k in range(2):
                    pool.wait_ge(y_done, it.no * 2 + k + 1)
                    if k == 0:
                        pool.wait_ge(added[1 - it.slot], (it.pair + it.slot) * 128)
                    carry_waits(it.no * 3 + k + (1 if last and it.slot == 1 else 2))
                    for g in range(4 * k, 4 * k + 4):
                        pool.indirect_dma_start(
                            out=out_rows[:, :], out_offset=bass.IndirectOffsetOnAxis(ap=idx[it.slot][:, g:g + 1], axis=0),
                            in_=y[it.slot][:, g, :], in_offset=None, bounds_check=last_token, oob_is_err=True,
                            compute_op=ALU.add).then_inc(added[it.slot], 16)

            all_experts(pool, step)
            for k in range(2):
                pool.wait_ge(added[k], E // 2 * 128)

        @block.vector
        def _(dve):
            for k in range(2):
                dve.wait_ge(turned, k + 1)
                dve.tensor_copy(lg_rows[:, k * HALF * C:(k + 1) * HALF * C], banks[k][:, 0:HALF * C]
                                ).then_inc(lg_copied, 1)
            dve.wait_ge(lg_copied, 2)
            dve.tensor_reduce(row_ends[:, 0:1], lg_rows[:, :], AX_X, ALU.max).then_inc(dve_step, 1)
            dve.tensor_reduce(row_ends[:, 1:2], lg_rows[:, :], AX_X, ALU.min).then_inc(dve_step, 1)
            dve.wait_ge(ends_turned, 1)
            for k, op in enumerate((ALU.max, ALU.min)):
                dve.tensor_reduce(ends[:, k, :], banks[2][0:1, k * 128:(k + 1) * 128].rearrange("p (b e) -> p e b", e=E),
                                  AX_X, op).then_inc(ends_done, 1)
            dve.wait_ge(ends_spread, 1)
            dve.tensor_copy(ends_all[:, :, :].rearrange("p k e -> p (k e)"), banks[3][:, 0:2 * E]).then_inc(dve_step, 1)
            dve.wait_ge(dve_step, 3)
            dve.tensor_tensor(ends_sel[:, :, :], ends_all[:, :, :],
                              const("expert_of").unsqueeze(1).broadcast_to([128, 2, E]), ALU.mult).then_inc(dve_step, 1)
            dve.tensor_scalar(neg_top[:, 1:1 + E], ends_all[:, 0, :], -1.0, None, ALU.mult)
            dve.wait_ge(dve_step, 4)
            dve.tensor_reduce(top_low[:, :], ends_sel[:, :, :], AX_X, ALU.add).then_inc(dve_step, 1)
            dve.wait_ge(dve_step, 5)
            dve.tensor_scalar(neg_top[:, 0:1], top_low[:, 0:1], -1.0, None, ALU.mult).then_inc(top_done, 1)
            dve.tensor_tensor(width[:, :], top_low[:, 0:1], top_low[:, 1:2], ALU.subtract).then_inc(dve_step, 1)
            dve.tensor_copy(low[:, :], top_low[:, 1:2])
            dve.wait_ge(dve_step, 6)
            dve.tensor_scalar(width[:, :], width[:, :], 0.25, None, ALU.mult).then_inc(dve_step, 1)
            dve.wait_ge(dve_step, 7)
            dve.scalar_tensor_tensor(thresholds[:, :], const("k_of"), width[:, 0:1], low[:, 0:1].broadcast_to([128, 3]),
                                     ALU.mult, ALU.add).then_inc(thresholds_set, 1)
            dve.wait_ge(exp_done, 1)
            dve.tensor_scalar(exp_sums[:, :], const("expert_of"), exp_sum[:, 0:1], None, ALU.mult).then_inc(exp_sums_done, 1)
            dve.wait_ge(sums_spread, 1)
            dve.reciprocal(inv_sum[:, :], banks[4][:, 0:E])
            with dve.Fori(0, ROUNDS) as r:
                dve.wait_ge(thresholds_set, r + 1)
                for k in range(2):
                    if k:
                        dve.wait_ge(counted_dve, r * 2 + 1)
                    dve.tensor_scalar(scratch[:, :], lg_rows[:, :], thresholds[:, k:k + 1], None, ALU.is_lt, ALU.add,
                                      accum_out=counts[:, k:k + 1]).then_inc(counted_dve, 1)
                dve.wait_ge(totals_done, r + 1)
                dve.tensor_tensor(passed[:, :], banks[5][:, 0:3], const("bound"), ALU.is_le).then_inc(round_step, 1)
                dve.wait_ge(round_step, r * 4 + 1)
                dve.tensor_reduce(n_passed[:, :], passed[:, :], AX_X, ALU.add).then_inc(round_step, 1)
                dve.wait_ge(round_step, r * 4 + 2)
                dve.scalar_tensor_tensor(low[:, :], n_passed[:, :], width[:, 0:1], low[:, :], ALU.mult,
                                         ALU.add).then_inc(round_step, 1)
                dve.wait_ge(round_step, r * 4 + 3)
                dve.tensor_scalar(width[:, :], width[:, :], 0.25, None, ALU.mult).then_inc(round_step, 1)
                dve.wait_ge(round_step, r * 4 + 4)
                dve.scalar_tensor_tensor(thresholds[:, :], const("k_of"), width[:, 0:1],
                                         low[:, 0:1].broadcast_to([128, 3]), ALU.mult, ALU.add).then_inc(thresholds_set, 1)
            dve.scalar_tensor_tensor(high[:, :], width[:, :], 4.0, low[:, :], ALU.mult, ALU.add).then_inc(dve_step, 1)
            dve.wait_ge(dve_step, 8)
            dve.tensor_scalar(sure[:, :], lg_rows[:, :], high[:, 0:1], None, ALU.is_gt, ALU.add,
                              accum_out=row_counts[:, 0:1]).then_inc(dve_step, 1)
            dve.wait_ge(dve_step, 9)
            dve.scalar_tensor_tensor(band[:, :], lg_rows[:, :], low[:, 0:1], sure[:, :], ALU.is_ge,
                                     ALU.subtract).then_inc(dve_step, 1)
            dve.wait_ge(dve_step, 10)
            dve.tensor_reduce(row_counts[:, 1:2], band[:, :], AX_X, ALU.add).then_inc(rows_counted, 1)
            dve.wait_ge(offsets_done, 1)
            dve.tensor_copy(offsets[:, :], banks[6][:, 0:3]).then_inc(dve_step, 1)
            dve.wait_ge(dve_step, 11)
            dve.tensor_tensor(offsets[:, 1:2], offsets[:, 1:2], offsets[:, 2:3], ALU.add).then_inc(dve_step, 1)
            dve.memset(scratch[:, :], 1.0).then_inc(dve_step, 1)
            dve.wait_ge(dve_step, 13)
            dve.tensor_tensor_scan(sure_rank[:, :], scratch[:, :], sure[:, :], offsets[:, 0:1], ALU.mult, ALU.add)
            dve.tensor_tensor_scan(band_rank[:, :], scratch[:, :], band[:, :], offsets[:, 1:2], ALU.mult,
                                   ALU.add).then_inc(dve_step, 1)
            dve.wait_ge(dve_step, 14)
            dve.tensor_tensor(sure_rank[:, :], sure_rank[:, :], sure[:, :], ALU.mult)
            dve.tensor_tensor(band_rank[:, :], band_rank[:, :], band[:, :], ALU.mult).then_inc(dve_step, 1)
            dve.wait_ge(dve_step, 15)
            dve.scalar_tensor_tensor(place[:, :], sure_rank[:, :], -1.0, band_rank[:, :], ALU.add,
                                     ALU.add).then_inc(place_done, 1)
            for k, (lo, hi) in enumerate(((0, 4), (4, NC))):
                dve.wait_ge(place_turned, k + 1)
                dve.tensor_copy(place_tok[:, :, lo * B:hi * B].rearrange("p e (c b) -> p c b e", b=B),
                                banks[k][0:C, 0:(hi - lo) * 128].rearrange("p (c b e) -> p c b e", b=B, e=E)
                                ).then_inc(split_step, 1)
            dve.wait_ge(split_step, 2)
            dve.tensor_scalar(place_int[:, :, :], place_tok[:, :, :], 7, None, ALU.arith_shift_right).then_inc(split_step, 1)
            dve.wait_ge(split_step, 3)
            dve.tensor_copy(block16[:, :, :], place_int[:, :, :]).then_inc(split_step, 1)
            dve.wait_ge(split_step, 4)
            dve.tensor_scalar(place_int[:, :, :], place_tok[:, :, :], 127, None, ALU.bitwise_and).then_inc(split_step, 1)
            dve.wait_ge(split_step, 5)
            dve.tensor_copy(slot16[:, :, :], place_int[:, :, :]).then_inc(split_step, 1)
            dve.wait_ge(split_step, 6)

            dve.tensor_copy(numbers16[:, :], const("numbers")).then_inc(split_step, 1)
            dve.wait_ge(split_step, 7)
            slot_nos = numbers16[0:C, 0:128].unsqueeze(1).broadcast_to([C, TILES, 128])
            block_nos = numbers16[0:C, 128:128 + G].unsqueeze(1).broadcast_to([C, TILES, G])
            tile_nos = numbers16[0:C, 128 + G:128 + G + TILES].unsqueeze(2).broadcast_to([C, TILES, G])

            def hot(it):
                if not early(it, 2):
                    dve.wait_ge(idx_ps, it.no - 1)
                mine = bass.ds(it.no, 1)
                dve.tensor_tensor(slot_hot[it.slot][:, :, :], slot_nos,
                                  slot16[:, mine, :].rearrange("p a t -> p (a t)").unsqueeze(2).broadcast_to([C, TILES, 128]),
                                  ALU.is_equal)
                dve.wait_ge(hot_done, it.no)
                dve.tensor_tensor(block_hot[:, :, :], block_nos,
                                  block16[:, mine, :].rearrange("p a t -> p (a t)").unsqueeze(2).broadcast_to([C, TILES, G]),
                                  ALU.is_equal).then_inc(hot_step, 1)
                dve.wait_ge(hot_step, it.no + 1)
                dve.tensor_scalar(block_val[it.slot][:, :, 0:G], block_hot[:, :, :], const("partition", C), None, ALU.mult)
                dve.tensor_tensor(block_val[it.slot][:, :, G:2 * G], block_hot[:, :, :], tile_nos,
                                  ALU.mult).then_inc(hot_done, 1)

            def list_out(it):
                dve.wait_ge(idx_ps, it.no + 1)
                dve.tensor_scalar(idx_tile[:, :], ps_idx[:, G:2 * G], float(C), None, ALU.mult).then_inc(idx_step, 1)
                if not early(it, 2):
                    dve.wait_ge(added[it.slot], it.pair * 128)
                dve.wait_ge(idx_step, it.no + 1)
                dve.tensor_tensor(idx[it.slot][:, :], idx_tile[:, :], ps_idx[:, 0:G], ALU.add).then_inc(idx_done, 1)

            hot(item(0))
            hot(item(1))
            list_out(item(0))

            def step(it, last):
                if not (last and it.slot == 1):
                    after = Item(it.no + 1, it.pair + it.slot, 1 - it.slot)
                    list_out(after)
                if not last:
                    hot(Item(it.no + 2, it.pair + 1, it.slot))
                dve.wait_ge(y_done, it.no * 2)
                dve.wait_ge(weight_step, it.no + 1)
                dve.tensor_scalar(weight[:, :], weight_exp[:, :], inv_sum[:, bass.ds(it.no, 1)], None,
                                  ALU.mult).then_inc(weight_done, 1)
                for k in range(2):
                    dve.wait_ge(y_ps, it.no * 2 + k + 1)
                    dve.tensor_tensor(y_sum[:, 4 * k:4 * k + 4, :], ps_Y[k][:, :].rearrange("p (g d) -> p g d", d=D),
                                      b2_sb[it.slot][:, :].unsqueeze(1).broadcast_to([128, 4, D]), ALU.add
                                      ).then_inc(y_step, 1)
                    dve.wait_ge(y_step, it.no * 2 + k + 1)
                    if not early(it, 2) and k == 0:
                        dve.wait_ge(added[it.slot], it.pair * 128)
                    dve.tensor_tensor(y[it.slot][:, 4 * k:4 * k + 4, :], y_sum[:, 4 * k:4 * k + 4, :],
                                      weight[:, 4 * k:4 * k + 4].unsqueeze(2).broadcast_to([128, 4, D]), ALU.mult
                                      ).then_inc(y_done, 1)

            all_experts(dve, step)


_INS = ["x", "L0_tok_W_ve", "L0_tok_b_ve", "L0_tok_W_lin", "L0_tok_b_lin", "L0_attn_wq", "L0_attn_bq", "L0_attn_wk",
        "L0_attn_bk", "L0_attn_wv", "L0_attn_bv", "L0_attn_wg", "L0_attn_bg", "L0_ffn_Wr", "L0_ffn_W1", "L0_ffn_b1",
        "L0_ffn_W2", "L0_ffn_b2"]


def kernel(**inputs):
    import concourse.bacc as bacc
    from concourse.bass_utils import run_bass_kernel_spmd

    nc = bacc.Bacc("TRN2", target_bir_lowering=False, num_devices=1)
    data = {name: np.ascontiguousarray(inputs[name]) for name in _INS}
    data["L0_ffn_W1"] = np.ascontiguousarray(
        data["L0_ffn_W1"].reshape(E, D, 128, FT).transpose(0, 1, 3, 2).reshape(E, D, F))
    data["consts"] = constants()
    arrays, args = {}, []
    for name, a in data.items():
        arrays[f"in_{name}"] = a
        args.append(nc.dram_tensor(f"in_{name}", a.shape, mybir.dt.from_np(a.dtype), kind="ExternalInput").ap())
    args.append(nc.dram_tensor("out", (B, T, D), F32, kind="ExternalOutput").ap())
    program(nc, *args)
    r = run_bass_kernel_spmd(nc, [arrays], core_ids=[0])
    return r.results[0]["out"]
```

```python
from contextlib import ExitStack

import numpy as np

import concourse.bass as bass
from concourse import mybir

F32 = mybir.dt.float32
BF16 = mybir.dt.bfloat16
I32 = mybir.dt.int32
U32 = mybir.dt.uint32
ALU = mybir.AluOpType
ACT = mybir.ActivationFunctionType
AX_X = mybir.AxisListType.X

B, CH, T, D = 16, 32, 750, 128
H, DH = 8, 16
C = 125
NC = T // C
HALF = NC // 2
N = B * T
E, F, CAP = 8, 512, 1024
FT = F // 128
G = CAP // 128
TILES = N // C
RUN = 4
RUNS = TILES // RUN
ROW = D + E
ALPHA = 0.1
EPS = 1e-5
ROUNDS = 16


class Item:

    def __init__(self, no, pair, slot):
        self.no, self.pair, self.slot = no, pair, slot


def item(no):
    return Item(no, no // 2, no % 2)


UNITS = ["x0", "x1", "o0", "o1", "q0", "a5", "q1", "k0", "k1", "a4", "g0", "g1", "t0", "t1", "a3",
         "v0", "v1", "v2", "a2", "h0", "h1", "b0", "b1", "a1", "s0", "s1", "lg", "a0"]
BANKS = 4
OF_ITEM = {"o": -1, "b": -1, "l": -1, "a": 0, "h": 2}


def bank_of(unit):
    return UNITS.index(unit) % BANKS


def before_in_bank(step, unit):
    at = UNITS.index(unit)
    while True:
        at -= BANKS
        if at < 0:
            at, step = at + len(UNITS), step - 1
        if isinstance(step, int) and step < -2:
            return None, None
        former = UNITS[at]
        no = step + OF_ITEM.get(former[0], 1)
        if not isinstance(no, int) or 0 <= no < B:
            return former, no


def early(it, n):
    return it is not None and isinstance(it.no, int) and it.no < n


CONSTS = {}


def constants():
    p = np.arange(128)
    head = p // DH
    gamma = 1.0 - 2.0 ** (-5.0 - head.astype(np.float64))
    i = np.arange(C)
    parts = {
        "ident": np.eye(128),
        "keep": (p[:, None] >= i[None, :]),
        "q_decay": gamma[:, None] ** (-i[None, :]) / np.sqrt(DH),
        "k_decay": gamma[:, None] ** i[None, :],
        "chunk_decay": gamma[:, None] ** C,
        "odd_head": (head[:, None] % 2 == 1),
        "block_decay": (head[:, None] == head[None, :]) * gamma[:, None] ** C,
        "same_expert": (p[:, None] % E == p[None, :] % E),
        "earlier_row": (p[:, None] % E == p[None, :] % E) & (p[:, None] // E < p[None, :] // E),
        "expert_of": (p[:, None] % E == np.arange(E)[None, :]),
        "ones": np.ones((128, 128)),
        "k_of": np.broadcast_to(np.arange(1, 4)[None, :], (128, 3)),
        "bound": np.broadcast_to(np.array([N - CAP, N - CAP, N - 2 * CAP])[None, :], (128, 3)),
        "partition": p[:, None],
        "even_odd": np.concatenate([np.broadcast_to(head % 2 == k, (128, 128)) for k in range(2)], axis=1),
        "half": np.full((128, NC), -0.5),
        "numbers": np.broadcast_to(np.concatenate([
            np.repeat(np.arange(128), RUN), np.repeat(np.arange(G), RUN),
            (np.arange(B)[None, :] * NC + np.arange(NC)[:, None]).reshape(-1)])[None, :],
            (128, (128 + G) * RUN + TILES)),
    }
    at = 0
    cols = []
    for name, a in parts.items():
        CONSTS[name] = (at, a.shape[1])
        at += a.shape[1]
        cols.append(a.astype(np.float32))
    return np.ascontiguousarray(np.concatenate(cols, axis=1))


def program(nc, x, w_ve, b_ve, w_lin, b_lin, wq, bq, wk, bk, wv, bv, wg, bg, wr, w1, b1, w2, b2,
            consts, out):
    constants()
    smooth_dram = nc.dram_tensor("smooth_dram", (B, CH, T), F32).ap()
    rows_dram = nc.dram_tensor("rows_dram", (N, ROW), F32).ap()
    out_rows = out.rearrange("b t d -> (b t) d")
    x_rows = x.rearrange("b c t -> (b c) t")
    smooth_rows = smooth_dram.rearrange("b c t -> (b c) t")
    out_items = out.rearrange("b (c p) d -> b p c d", p=C)
    row_items = rows_dram.rearrange("(b c p) d -> b p c d", c=NC, p=C)

    with ExitStack() as ctx:
        def sb(name, shape, dt=F32):
            return ctx.enter_context(nc.sbuf_tensor(name, shape, dt))

        def psum(name, shape, dt=F32):
            return ctx.enter_context(nc.psum_tensor(name, shape, dt))

        def sem(name):
            return ctx.enter_context(nc.semaphore(name))

        cst = sb("cst", [128, consts.shape[1]])
        numbers16 = sb("numbers16", [128, (128 + G) * RUN + TILES], BF16)

        def const(name, rows=128):
            at, n = CONSTS[name]
            return cst[0:rows, at:at + n]

        ident = const("ident")

        logits = sb("logits", [C, NC, B * E])
        w_col = sb("w_col", [128, 3])
        v_bias = sb("v_bias", [C, D])
        wr_wide = sb("wr_wide", [D, D])
        wT = sb("wT", [D, 4, D])
        emb_w = sb("emb_w", [CH + 1, D])
        weight_in = sb("weight_in", [D, 5, D])
        ve_in = sb("ve_in", [D, CH])
        bve_in = sb("bve_in", [D, 1])
        lin_T = sb("lin_T", [D, D])
        blin_in = sb("blin_in", [1, D])

        stage1 = ExitStack()

        def s1(name, shape, dt=F32):
            return stage1.enter_context(nc.sbuf_tensor(name, shape, dt))

        xin = s1("xin", [128, 4, T])
        diff = s1("diff", [128, T])
        scaled = s1("scaled", [128, T])
        fwd = s1("fwd", [128, T])
        bwd = s1("bwd", [128, T])
        smooth = s1("smooth", [128, 4, T])
        keep9 = s1("keep9", [128, T])
        s_in = [s1(f"s_in{k}", [CH + 1, T]) for k in range(2)]
        h_sb = [s1(f"h_sb{k}", [C, NC, D]) for k in range(2)]
        h_kept = s1("h_kept", [C, NC, D])
        h2_sb = [s1(f"h2_sb{k}", [C, NC, D]) for k in range(2)]
        stats = s1("stats", [C, NC, 6])
        moments = s1("moments", [C, NC, 2])
        rstd = s1("rstd", [C, NC])
        xn = s1("xn", [C, NC, D])
        xT = [s1(f"xT{k}", [D, T]) for k in range(2)]
        q_dec = [s1(f"q_dec{k}", [D, T]) for k in range(2)]
        q_odd = [s1(f"q_odd{k}", [D, T]) for k in range(2)]
        k_dec = [s1(f"k_dec{k}", [D, T]) for k in range(2)]
        k_tok = [s1(f"k_tok{k}", [C, NC, D]) for k in range(2)]
        v_split = [s1(f"v_split{k}", [C, NC, 2, D]) for k in range(2)]
        v_tok = [s1(f"v_tok{k}", [C, NC, D]) for k in range(2)]
        gate = [s1(f"gate{k}", [D, T]) for k in range(2)]
        prob = [s1(f"prob{k}", [C, H, C]) for k in range(2)]
        attn = s1("attn", [D, T])
        state = [s1(f"state{k}", [D, NC - 1, D]) for k in range(2)]
        stats2 = s1("stats2", [C, NC, 6])
        moments2 = s1("moments2", [C, NC, 2])
        rstd2 = s1("rstd2", [C, NC])
        row_sb = [s1(f"row_sb{k}", [C, NC, ROW]) for k in range(2)]
        x2T = s1("x2T", [D, T])

        def p1(name, shape):
            return stage1.enter_context(nc.psum_tensor(name, shape, F32))

        bank = [p1(f"bank{k}", [128, 512]) for k in range(BANKS)]
        ps_score = p1("ps_score", [128, 4, 512])

        consts_in = sem("consts_in")
        x_in = [sem(f"x_in{k}") for k in range(4)]
        scan_step = sem("scan_step")
        smooth_done = sem("smooth_done")
        smooth_out = sem("smooth_out")
        setup_pe = sem("setup_pe")
        setup_act = sem("setup_act")
        ones_set = sem("ones_set")
        s_loaded = [sem(f"s_loaded{k}") for k in range(2)]
        filled = {u: sem(f"filled_{u}") for u in UNITS}
        read = {u: sem(f"read_{u}") for u in UNITS}
        stats_done = sem("stats_done")
        moments_step = sem("moments_step")
        rstd_done = sem("rstd_done")
        xn_done = sem("xn_done")
        q_odd_done = sem("q_odd_done")
        low_scored = sem("low_scored")
        high_scored = sem("high_scored")
        low_masked = sem("low_masked")
        high_copied = sem("high_copied")
        high_masked = sem("high_masked")
        state_step = sem("state_step")
        state_done = sem("state_done")
        stats2_done = sem("stats2_done")
        moments2_step = sem("moments2_step")
        rstd2_done = sem("rstd2_done")
        xn2_done = sem("xn2_done")
        logits_done = sem("logits_done")
        v_split_done = sem("v_split_done")
        h_moved = sem("h_moved")
        h2_out = [sem(f"h2_out{k}") for k in range(2)]
        rows_out = [sem(f"rows_out{k}") for k in range(2)]
        stage1_block = nc.Block()
        stage1.enter_context(stage1_block)
        block = stage1_block

        def chunk(c):
            return slice(c * C, (c + 1) * C)

        def items_of_loop(i, odd):
            if odd:
                return (i * 2 + 1, Item(i * 2, i, 0), Item(i * 2 + 1, i, 1), Item(i * 2 + 2, i + 1, 0),
                        Item(i * 2 + 3, i + 1, 1))
            return (i * 2, Item(i * 2 - 1, i - 1, 1), Item(i * 2, i, 0), Item(i * 2 + 1, i, 1),
                    Item(i * 2 + 2, i + 1, 0))

        def all_steps(eng, step):
            def single(n):
                step(n, *(item(k) if 0 <= k < B else None for k in range(n - 1, n + 3)))

            for n in range(-2, 4):
                single(n)
            with eng.Fori(2, B // 2 - 1) as i:
                for odd in range(2):
                    step(*items_of_loop(i, odd))
            for n in range(B - 2, B + 1):
                single(n)

        def prob_free(eng, own, c):
            if c < NC - 2:
                eng.wait_ge(filled[f"a{c + 2}"], own.no + 1)
            elif not early(own, 1):
                eng.wait_ge(filled[f"a{c + 2 - NC}"], own.no)

        @block.sync
        def _(sp):
            sp.dma_start(cst[:, :], consts).then_inc(consts_in, 16)
            for k, (dst, src) in enumerate([
                    (weight_in[:, 4, :], w_lin), (ve_in[:, :], w_ve), (bve_in[:, :], b_ve.unsqueeze(1)),
                    (blin_in[:, :], b_lin.unsqueeze(0)),
                    (weight_in[:, 0, :], wq), (weight_in[:, 1, :], wk), (weight_in[:, 2, :], wv),
                    (weight_in[:, 3, :], wg), (w_col[:, 0:1], bq.unsqueeze(1)), (w_col[:, 1:2], bk.unsqueeze(1)),
                    (v_bias[:, :], bv.unsqueeze(0).broadcast_to([C, D])),
                    (w_col[:, 2:3], bg.unsqueeze(1)),
                    (wr_wide[:, 0:E], wr)]):
                sp.dma_start(dst, src).then_inc(consts_in, 16)
            def smooth_part(j):
                sp.wait_ge(smooth_done, j + 1)
                sp.dma_start(smooth_rows[j * 128:(j + 1) * 128, :], smooth[:, j, :]).then_inc(smooth_out, 16)

            smooth_part(0)

            def step(n, before, own, after, coming):
                if coming:
                    if early(coming, 1):
                        sp.wait_ge(smooth_out, 16)
                    elif early(coming, 5) and not early(coming, 4):
                        sp.wait_ge(smooth_out, 64)
                    if not early(coming, 2):
                        sp.wait_ge(filled["h1"], coming.no - 1)
                    sp.dma_start(s_in[coming.slot][0:CH, :],
                                 smooth_dram[bass.ds(coming.no, 1)].rearrange("a c t -> (a c) t")
                                 ).then_inc(s_loaded[coming.slot], 16)
                    if early(coming, 3):
                        smooth_part(coming.no + 1)
                if before:
                    sp.wait_ge(read["o1"], before.no + 1)
                    sp.dma_start(out_items[bass.ds(before.no, 1)].rearrange("a p c d -> (a p) c d"),
                                 h2_sb[before.slot][:, :, :]).then_inc(h2_out[before.slot], 16)
                    sp.wait_ge(xn2_done, before.no + 1)
                    sp.wait_ge(logits_done, before.no + 1)
                    sp.dma_start(row_items[bass.ds(before.no, 1)].rearrange("a p c d -> (a p) c d"),
                                 row_sb[before.slot][:, :, :]).then_inc(rows_out[before.slot], 16)

            all_steps(sp, step)
            for k in range(2):
                sp.wait_ge(h2_out[k], 16 * B // 2)
                sp.wait_ge(rows_out[k], 16 * B // 2)

        @block.tensor
        def _(pe):
            pe.wait_ge(consts_in, 16 * 14)
            pe.transpose(bank[0][:, 0:D], weight_in[:, 4, :], ident).then_inc(setup_pe, 1)
            for k in range(4):
                t = pe.transpose(bank[1][:, k * D:(k + 1) * D], weight_in[:, k, :], ident)
            t.then_inc(setup_pe, 1)
            pe.wait_ge(setup_act, 1)
            pe.matmul(bank[2][0:CH, 0:D], ve_in[:, :], lin_T[:, :], start=True, stop=True)
            pe.matmul(bank[2][CH:CH + 1, D:2 * D], bve_in[:, :], lin_T[:, :], start=True, stop=False,
                      skip_group_check=True)
            pe.matmul(bank[2][CH:CH + 1, D:2 * D], const("ones")[0:1, 0:1], blin_in[:, :], start=False, stop=True,
                      skip_group_check=True).then_inc(setup_pe, 1)
            pe.wait_ge(setup_act, 4)

            def claim(step, unit):
                former, no = before_in_bank(step, unit)
                if former:
                    pe.wait_ge(read[former], no + 1)
                return bank[bank_of(unit)]

            def scores(own, c):
                done = own.no * NC + (NC - 1 - c)
                if c == NC - 1:
                    pe.wait_ge(read["q1"], own.no + 1)
                    pe.wait_ge(q_odd_done, own.no + 1)
                    pe.wait_ge(read["k1"], own.no + 1)
                pe.wait_ge(low_masked, done)
                pe.wait_ge(high_copied, done)
                for h in (0, 2, 4, 6, 1, 3, 5, 7):
                    g, lo = h // 2, 32 * (h // 2)
                    rows = slice(lo, lo + 32) if h % 2 else slice(lo, lo + DH)
                    q = (q_odd if h % 2 else q_dec)[own.slot]
                    at = (h % 2) * C
                    m = pe.matmul(ps_score[0:C, g, at:at + C], k_dec[own.slot][rows, chunk(c)], q[rows, chunk(c)],
                                  start=True, stop=True)
                    if h == 3:
                        m.then_inc(low_scored, 1)
                m.then_inc(high_scored, 1)

            def values(own, c):
                unit = f"a{c}"
                o = claim(own.no, unit)[:, 0:C]
                if c == NC - 1:
                    pe.wait_ge(state_done, own.no + 1)
                    pe.wait_ge(v_split_done, own.no * 2 + 2)
                else:
                    pe.matmul(o, state[own.slot][:, c, :], q_dec[own.slot][:, chunk(c)], start=True, stop=False,
                              skip_group_check=True)
                pe.wait_ge(low_masked, own.no * NC + (NC - c))
                pe.wait_ge(high_masked, own.no * NC + (NC - c))
                for k, h in enumerate((0, 2, 4, 6, 1, 3, 5, 7)):
                    rows = slice(h // 2 * 32, h // 2 * 32 + 32)
                    m = pe.matmul(o[rows, :], v_split[own.slot][:, c, h % 2, rows], prob[c % 2][:, h, :],
                                  start=(c == NC - 1 and k < 4), stop=(k >= 4), skip_group_check=True)
                m.then_inc(filled[unit], 1)

            def step(n, before, own, after, coming):
                def h_units():
                    if early(coming, 1):
                        pe.wait_ge(ones_set, 1)
                    pe.wait_ge(s_loaded[coming.slot], coming.pair * 16 + 16)
                    for k in range(2):
                        ps = claim(n, f"h{k}")
                        for c in range(HALF):
                            m = pe.matmul(ps[0:C, c * D:(c + 1) * D], s_in[coming.slot][:, chunk(k * HALF + c)],
                                          emb_w[:, :], start=True, stop=True)
                        m.then_inc(filled[f"h{k}"], 1)

                def x_units():
                    pe.wait_ge(xn_done, after.no + 1)
                    for k in range(2):
                        ps = claim(n, f"x{k}")
                        for c in range(HALF):
                            m = pe.transpose(ps[:, chunk(c)], xn[:, k * HALF + c, :], ident[0:C, 0:C])
                        m.then_inc(filled[f"x{k}"], 1)

                def o_units():
                    for k in range(2):
                        pe.wait_ge(read["a0"], before.no + 1)
                        ps = claim(n, f"o{k}")
                        for c in range(HALF):
                            m = pe.transpose(ps[0:C, c * D:(c + 1) * D], attn[:, chunk(k * HALF + c)], ident)
                        m.then_inc(filled[f"o{k}"], 1)

                def project(name, w, ks=(0, 1)):
                    for k in ks:
                        ps = claim(n, f"{name}{k}")
                        pe.wait_ge(read[f"x{k}"], after.no + 1)
                        pe.matmul(ps[:, 0:HALF * C], wT[:, w, :], xT[after.slot][:, k * HALF * C:(k + 1) * HALF * C],
                                  start=True, stop=True).then_inc(filled[f"{name}{k}"], 1)

                def k_tok_units():
                    for k in range(2):
                        pe.wait_ge(read[f"k{k}"], after.no + 1)
                        ps = claim(n, f"t{k}")
                        for c in range(HALF):
                            m = pe.transpose(ps[0:C, c * D:(c + 1) * D], k_dec[after.slot][:, chunk(k * HALF + c)],
                                             ident)
                        m.then_inc(filled[f"t{k}"], 1)

                def v_units():
                    for k in range(3):
                        ps = claim(n, f"v{k}")
                        for c in range(2):
                            m = pe.matmul(ps[0:C, c * D:(c + 1) * D], xT[after.slot][:, chunk(2 * k + c)],
                                          wT[:, 2, :], start=True, stop=True)
                        m.then_inc(filled[f"v{k}"], 1)

                def state_units():
                    pe.wait_ge(read["t1"], after.no + 1)
                    pe.wait_ge(read["v2"], after.no + 1)
                    for k, cs in enumerate(([4, 3, 2, 1], [0])):
                        ps = claim(n, f"s{k}")
                        for c in cs:
                            at = (c - cs[-1]) * D
                            m = pe.matmul(ps[:, at:at + D], k_tok[after.slot][:, c + 1, :],
                                          v_tok[after.slot][:, c + 1, :], start=True, stop=True)
                        m.then_inc(filled[f"s{k}"], 1)

                def b_units():
                    pe.wait_ge(xn2_done, before.no + 1)
                    for k in range(2):
                        ps = claim(n, f"b{k}")
                        for c in range(HALF):
                            m = pe.transpose(ps[:, chunk(c)], row_sb[before.slot][:, k * HALF + c, 0:D],
                                             ident[0:C, 0:C])
                        m.then_inc(filled[f"b{k}"], 1)

                def logits_unit():
                    pe.wait_ge(read["b1"], before.no + 1)
                    ps = claim(n, "lg")
                    for c in range(NC):
                        m = pe.matmul(ps[0:C, c * E:c * E + D], x2T[:, chunk(c)], wr_wide[:, :], start=True, stop=True)
                    m.then_inc(filled["lg"], 1)

                if own:
                    scores(own, 5)
                if after:
                    x_units()
                if before:
                    o_units()
                if after:
                    project("q", 0, (0,))
                if own:
                    scores(own, 4)
                    values(own, 5)
                if after:
                    project("q", 0, (1,))
                    project("k", 1)
                if own:
                    scores(own, 3)
                    values(own, 4)
                if after:
                    project("g", 3)
                    k_tok_units()
                if own:
                    scores(own, 2)
                    values(own, 3)
                if after:
                    v_units()
                if own:
                    scores(own, 1)
                    values(own, 2)
                if coming:
                    h_units()
                if before:
                    b_units()
                if own:
                    scores(own, 0)
                    values(own, 1)
                if after:
                    state_units()
                if before:
                    logits_unit()
                if own:
                    values(own, 0)

            all_steps(pe, step)

        @block.scalar
        def _(act):
            act.dma_start(xin[:, 0, :], x_rows[0:128, :]).then_inc(x_in[0], 16)
            for j in range(1, 4):
                act.dma_start(xin[:, j, :], x_rows[j * 128:(j + 1) * 128, :]).then_inc(x_in[j], 16)
            act.wait_ge(setup_pe, 1)
            act.copy(lin_T[:, :], bank[0][:, 0:D]).then_inc(setup_act, 1)
            act.wait_ge(setup_pe, 2)
            act.copy(wT[:, :, :].rearrange("p k d -> p (k d)"), bank[1][:, :]).then_inc(setup_act, 1)
            act.wait_ge(setup_pe, 3)
            act.copy(emb_w[0:CH, :], bank[2][0:CH, 0:D]).then_inc(setup_act, 1)
            act.copy(emb_w[CH:CH + 1, :], bank[2][CH:CH + 1, D:2 * D]).then_inc(setup_act, 1)

            def step(n, before, own, after, coming):
                def copy_out(it, unit, dst, rows, cols):
                    act.wait_ge(filled[unit], it.no + 1)
                    act.copy(dst, bank[bank_of(unit)][0:rows, 0:cols]).then_inc(read[unit], 1)

                def high_scores(c):
                    act.wait_ge(high_scored, own.no * NC + (NC - c))
                    prob_free(act, own, c)
                    act.copy(prob[c % 2][:, H // 2:H, :].rearrange("p (g e) i -> p g (e i)", e=2),
                             ps_score[0:C, 2:4, 0:2 * C]).then_inc(high_copied, 1)

                if own:
                    high_scores(5)
                if after:
                    if not early(after, 2):
                        act.wait_ge(filled["v2"], after.no - 1)
                    for k in range(2):
                        copy_out(after, f"x{k}", xT[after.slot][:, k * HALF * C:(k + 1) * HALF * C], D, HALF * C)
                if own:
                    high_scores(4)
                    if not early(own, 1):
                        act.wait_ge(read["o1"], own.no)
                    act.copy(h_kept[:, :, :], h_sb[own.slot][:, :, :]).then_inc(h_moved, 1)
                    high_scores(3)
                if after:
                    if not early(after, 2):
                        act.wait_ge(read["a0"], after.no - 1)
                    for k in range(2):
                        act.wait_ge(filled[f"g{k}"], after.no + 1)
                        act.activation(gate[after.slot][:, k * HALF * C:(k + 1) * HALF * C],
                                       bank[bank_of(f"g{k}")][:, 0:HALF * C], ACT.Silu,
                                       bias=w_col[:, 2:3]).then_inc(read[f"g{k}"], 1)
                    for k in range(2):
                        copy_out(after, f"t{k}", k_tok[after.slot][:, k * HALF:(k + 1) * HALF, :].rearrange("p c d -> p (c d)"),
                                 C, HALF * D)
                if own:
                    high_scores(2)
                    high_scores(1)
                if coming:
                    if not early(coming, 2):
                        act.wait_ge(h_moved, coming.no - 1)
                        act.wait_ge(xn_done, coming.no - 1)
                    for k in range(2):
                        copy_out(coming, f"h{k}", h_sb[coming.slot][:, k * HALF:(k + 1) * HALF, :].rearrange("p c d -> p (c d)"),
                                 C, HALF * D)
                if before:
                    if not early(before, 1):
                        act.wait_ge(filled["lg"], before.no)
                    for k in range(2):
                        copy_out(before, f"b{k}", x2T[:, k * HALF * C:(k + 1) * HALF * C], D, HALF * C)
                if own:
                    high_scores(0)

            all_steps(act, step)

        @block.gpsimd
        def _(pool):
            pool.memset(s_in[0][CH:CH + 1, :], 1.0)
            pool.memset(s_in[1][CH:CH + 1, :], 1.0).then_inc(ones_set, 1)
            pool.wait_ge(consts_in, 16 * 14)

            def step(n, before, own, after, coming):
                def high_mask(c):
                    done = own.no * NC + (NC - 1 - c)
                    pool.wait_ge(high_copied, done + 1)
                    p = prob[c % 2][:, H // 2:H, :]
                    pool.tensor_tensor(p, p, const("keep", C).unsqueeze(1).broadcast_to([C, H // 2, C]),
                                       ALU.mult).then_inc(high_masked, 1)

                def inverse_root(moments_ready, done, m, r):
                    pool.wait_ge(moments_ready, done)
                    return pool.tensor_tensor(r[:, :], m[:, :, 1], const("half", C), ALU.pow)

                def split_values(k):
                    if k == 0:
                        pool.wait_ge(read["v2"], after.no + 1)
                        if not early(after, 2):
                            pool.wait_ge(filled["a0"], after.no - 1)
                    cs = slice(k * HALF, (k + 1) * HALF)
                    pool.tensor_tensor(v_split[after.slot][:, cs, :, :],
                                       v_tok[after.slot][:, cs, :].unsqueeze(2).broadcast_to([C, HALF, 2, D]),
                                       const("even_odd", C).rearrange("p (w d) -> p w d", w=2).unsqueeze(1)
                                       .broadcast_to([C, HALF, 2, D]), ALU.mult).then_inc(v_split_done, 1)

                if own:
                    high_mask(5)
                    high_mask(4)
                    high_mask(3)
                if before:
                    inverse_root(moments2_step, 2 * before.no + 2, moments2, rstd2).then_inc(rstd2_done, 1)
                if own:
                    high_mask(2)
                if after:
                    pool.wait_ge(read["q0"], after.no + 1)
                    pool.wait_ge(read["q1"], after.no + 1)
                    pool.tensor_tensor(q_odd[after.slot][:, :], q_dec[after.slot][:, :],
                                       const("odd_head").broadcast_to([D, T]), ALU.mult).then_inc(q_odd_done, 1)
                if own:
                    high_mask(1)
                if after:
                    split_values(0)
                if coming:
                    inverse_root(moments_step, 2 * coming.no + 2, moments, rstd).then_inc(rstd_done, 1)
                if own:
                    high_mask(0)
                if after:
                    split_values(1)

            all_steps(pool, step)

        @block.vector
        def _(dve):
            dve.memset(wr_wide[:, E:D], 0.0)
            dve.memset(keep9[:, :], 1.0 - ALPHA)
            dve.memset(diff[:, 0:1], 0.0).then_inc(scan_step, 1)

            def smooth_part(j):
                dve.wait_ge(x_in[j], 16)
                if j:
                    dve.wait_ge(smooth_done, j)
                dve.tensor_tensor(diff[:, 1:T], xin[:, j, 1:T], xin[:, j, 0:T - 1], ALU.subtract).then_inc(scan_step, 1)
                dve.wait_ge(scan_step, 5 * j + 2)
                dve.tensor_scalar(scaled[:, :], diff[:, :], 0.5 * ALPHA, None, ALU.mult).then_inc(scan_step, 1)
                dve.wait_ge(scan_step, 5 * j + 3)
                dve.tensor_tensor_scan(fwd[:, :], keep9[:, :], scaled[:, :], 0.0, ALU.mult, ALU.add).then_inc(scan_step, 1)
                dve.wait_ge(scan_step, 5 * j + 4)
                dve.tensor_scalar(scaled[:, T - 1:T], diff[:, T - 1:T], 0.5, None, ALU.mult).then_inc(scan_step, 1)
                dve.wait_ge(scan_step, 5 * j + 5)
                dve.tensor_tensor_scan(bwd[:, ::-1], keep9[:, :], scaled[:, ::-1], 0.0, ALU.mult,
                                       ALU.add).then_inc(scan_step, 1)
                dve.wait_ge(scan_step, 5 * j + 6)
                dve.tensor_tensor(smooth[:, j, :], fwd[:, :], bwd[:, :], ALU.add).then_inc(smooth_done, 1)

            smooth_part(0)
            smooth_part(1)

            def step(n, before, own, after, coming):
                def low_scores(c):
                    dve.wait_ge(low_scored, own.no * NC + (NC - c))
                    prob_free(dve, own, c)
                    keep = const("keep", C).unsqueeze(1).unsqueeze(1).broadcast_to([C, 2, 2, C])
                    dve.tensor_tensor(prob[c % 2][:, 0:H // 2, :].rearrange("p (g e) i -> p g e i", e=2),
                                      ps_score[0:C, 0:2, 0:2 * C].rearrange("p g (e i) -> p g e i", e=2),
                                      keep, ALU.mult).then_inc(low_masked, 1)

                def states():
                    st = state[after.slot]
                    for k, (lo, hi) in enumerate(((1, NC - 1), (0, 1))):
                        dve.wait_ge(filled[f"s{k}"], after.no + 1)
                        dve.tensor_tensor(st[:, lo:hi, :],
                                          bank[bank_of(f"s{k}")][:, 0:(hi - lo) * D].rearrange("p (c d) -> p c d", d=D),
                                          const("block_decay").unsqueeze(1).broadcast_to([D, hi - lo, D]),
                                          ALU.mult).then_inc(read[f"s{k}"], 1)
                    dve.wait_ge(read["s1"], after.no + 1)
                    for k, c in enumerate(range(NC - 3, -1, -1)):
                        if k:
                            dve.wait_ge(state_step, after.no * (NC - 3) + k)
                        i = dve.scalar_tensor_tensor(st[:, c, :], st[:, c + 1, :], const("chunk_decay"), st[:, c, :],
                                                     ALU.mult, ALU.add)
                        i.then_inc(state_done if c == 0 else state_step, 1)

                def gated_out(c):
                    if c == NC - 1:
                        dve.wait_ge(read["g1"], own.no + 1)
                        if not early(own, 1):
                            dve.wait_ge(filled["o1"], own.no)
                    dve.wait_ge(filled[f"a{c}"], own.no + 1)
                    dve.tensor_tensor(attn[:, chunk(c)], bank[bank_of(f"a{c}")][:, 0:C], gate[own.slot][:, chunk(c)],
                                      ALU.mult).then_inc(read[f"a{c}"], 1)

                def residual():
                    if not early(before, 2):
                        dve.wait_ge(h2_out[before.slot], before.pair * 16)
                    dve.wait_ge(h_moved, before.no + 1)
                    for k in range(2):
                        cs = slice(k * HALF, (k + 1) * HALF)
                        dve.wait_ge(filled[f"o{k}"], before.no + 1)
                        dve.tensor_tensor(h2_sb[before.slot][:, cs, :],
                                          bank[bank_of(f"o{k}")][0:C, 0:HALF * D].rearrange("p (c d) -> p c d", d=D),
                                          h_kept[:, cs, :], ALU.add).then_inc(read[f"o{k}"], 1)

                def norm_stats(src, st, st_done, mo, mo_step, no):
                    for c in range(NC):
                        i = dve.bn_stats(st[:, c, :], src[:, c, :])
                    i.then_inc(st_done, 1)
                    dve.wait_ge(consts_in, 16 * 14)
                    dve.wait_ge(st_done, no + 1)
                    for c in range(NC):
                        i = dve.bn_aggr(mo[:, c, :], st[:, c, :])
                    i.then_inc(mo_step, 1)
                    dve.wait_ge(mo_step, 2 * no + 1)
                    dve.tensor_scalar(mo[:, :, 1], mo[:, :, 1], EPS, None, ALU.add).then_inc(mo_step, 1)

                def normalise(dst, src, mo, r, r_done, done, no):
                    dve.wait_ge(r_done, no + 1)
                    for c in range(NC):
                        i = dve.tensor_scalar(dst[:, c, 0:D], src[:, c, :], mo[:, c, 0:1], r[:, c:c + 1],
                                              ALU.subtract, ALU.mult)
                    i.then_inc(done, 1)

                def projected(unit, k, dst, bias, decay):
                    b = bank_of(unit)
                    dve.wait_ge(filled[unit], after.no + 1)
                    cols = slice(k * HALF * C, (k + 1) * HALF * C)
                    dve.scalar_tensor_tensor(
                        dst[:, cols].rearrange("p (c i) -> p c i", i=C),
                        bank[b][:, 0:HALF * C].rearrange("p (c i) -> p c i", i=C), bias,
                        decay.unsqueeze(1).broadcast_to([128, HALF, C]), ALU.add, ALU.mult).then_inc(read[unit], 1)

                if own:
                    low_scores(5)
                if before:
                    residual()
                if after:
                    if not early(after, 2):
                        dve.wait_ge(filled["a0"], after.no - 1)
                    projected("q0", 0, q_dec[after.slot], w_col[:, 0:1], const("q_decay"))
                if own:
                    low_scores(4)
                    gated_out(5)
                if after:
                    projected("q1", 1, q_dec[after.slot], w_col[:, 0:1], const("q_decay"))
                    for k in range(2):
                        projected(f"k{k}", k, k_dec[after.slot], w_col[:, 1:2], const("k_decay"))
                if own:
                    low_scores(3)
                    gated_out(4)
                if early(own, 1):
                    smooth_part(3)
                if before:
                    dve.wait_ge(read["o1"], before.no + 1)
                    norm_stats(h2_sb[before.slot], stats2, stats2_done, moments2, moments2_step, before.no)
                if own:
                    low_scores(2)
                    gated_out(3)
                if before:
                    if not early(before, 2):
                        dve.wait_ge(rows_out[before.slot], before.pair * 16)
                    normalise(row_sb[before.slot], h2_sb[before.slot], moments2, rstd2, rstd2_done, xn2_done,
                              before.no)
                if after:
                    for k in range(3):
                        dve.wait_ge(filled[f"v{k}"], after.no + 1)
                        dve.tensor_tensor(v_tok[after.slot][:, 2 * k:2 * k + 2, :],
                                          bank[bank_of(f"v{k}")][0:C, 0:2 * D].rearrange("p (c d) -> p c d", c=2),
                                          v_bias[:, :].unsqueeze(1).broadcast_to([C, 2, D]), ALU.add
                                          ).then_inc(read[f"v{k}"], 1)
                if own:
                    low_scores(1)
                    gated_out(2)
                if coming:
                    dve.wait_ge(read["h1"], coming.no + 1)
                    norm_stats(h_sb[coming.slot], stats, stats_done, moments, moments_step, coming.no)
                if own:
                    low_scores(0)
                    gated_out(1)
                if coming:
                    if not early(coming, 1):
                        dve.wait_ge(filled["x1"], coming.no)
                    normalise(xn, h_sb[coming.slot], moments, rstd, rstd_done, xn_done, coming.no)
                    if early(coming, 1):
                        smooth_part(2)
                if after:
                    states()
                if before:
                    dve.wait_ge(filled["lg"], before.no + 1)
                    lg = bank[bank_of("lg")][0:C, 0:NC * E].rearrange("p (c e) -> p c e", e=E)
                    dve.tensor_copy(row_sb[before.slot][:, :, D:ROW], lg).then_inc(logits_done, 1)
                    dve.tensor_copy(logits[:, :, bass.ds(before.no * E, E)], lg).then_inc(read["lg"], 1)
                if own:
                    gated_out(0)

            all_steps(dve, step)
        stage1.close()

        def s2(name, shape, dt=F32):
            return ctx.enter_context(nc.sbuf_tensor(name, shape, dt))

        lg_rows = s2("lg_rows", [128, T])
        scratch = s2("scratch", [128, T])
        scratch_act = s2("scratch_act", [128, T])
        row_ends = s2("row_ends", [128, 2])
        ends = s2("ends", [1, 2, E])
        ends_all = s2("ends_all", [128, 2, E])
        ends_sel = s2("ends_sel", [128, 2, E])
        top_low = s2("top_low", [128, 2])
        neg_top = s2("neg_top", [128, 1 + E])
        exp_sum = s2("exp_sum", [128, 1])
        exp_sums = s2("exp_sums", [128, E])
        inv_sum = s2("inv_sum", [128, E])
        low = s2("low", [128, 1])
        width = s2("width", [128, 1])
        thresholds = s2("thresholds", [128, 3])
        counts = s2("counts", [128, 3])
        passed = s2("passed", [128, 3])
        n_passed = s2("n_passed", [128, 1])
        high = s2("high", [128, 1])
        sure = s2("sure", [128, T])
        band = s2("band", [128, T])
        row_counts = s2("row_counts", [128, 2])
        offsets = s2("offsets", [128, 3])
        sure_rank = s2("sure_rank", [128, T])
        band_rank = s2("band_rank", [128, T])
        place = s2("place", [128, T])
        place_tok = s2("place_tok", [C, E, TILES], I32)
        place_int = s2("place_int", [C, E, TILES], I32)
        block16 = s2("block16", [C, E, TILES], BF16)
        slot16 = s2("slot16", [C, E, TILES], BF16)
        slot_hot = [s2(f"slot_hot{k}", [C, RUNS, 128, RUN], BF16) for k in range(2)]
        block_hot = s2("block_hot", [C, RUNS, G, RUN], BF16)
        block_val = [s2(f"block_val{k}", [C, RUNS, 2 * G, RUN], BF16) for k in range(2)]
        carrier = s2("carrier", [1, 1])
        idx_tile = s2("idx_tile", [128, G])
        idx = [s2(f"idx{k}", [128, G], U32) for k in range(2)]
        idx_add = [s2(f"idx_add{k}", [128, G], U32) for k in range(2)]
        taken = [s2(f"taken{k}", [128, G, ROW]) for k in range(2)]
        takenT = s2("takenT", [D, CAP])
        hidden = s2("hidden", [128, FT, CAP])
        weight_exp = s2("weight_exp", [128, G])
        weight = s2("weight", [128, G])
        y_sum = s2("y_sum", [128, G, D])
        y = [s2(f"y{k}", [128, G, D]) for k in range(2)]
        w1_sb = [s2(f"w1_sb{k}", [D, F]) for k in range(2)]
        w2_sb = [s2(f"w2_sb{k}", [128, FT, D]) for k in range(2)]
        b1_sb = [s2(f"b1_sb{k}", [128, FT]) for k in range(2)]
        b2_sb = [s2(f"b2_sb{k}", [128, D]) for k in range(2)]

        banks = [psum(f"bank2_{k}", [128, 512]) for k in range(8)]
        ps_idx, ps_T, ps_H, ps_Y = banks[0], banks[1:3], banks[3:6], banks[6:8]

        turned = sem("turned")
        lg_copied = sem("lg_copied")
        dve_step = sem("dve_step")
        ends_turned = sem("ends_turned")
        ends_done = sem("ends_done")
        ends_spread = sem("ends_spread")
        top_done = sem("top_done")
        exp_done = sem("exp_done")
        exp_sums_done = sem("exp_sums_done")
        sums_spread = sem("sums_spread")
        thresholds_set = sem("thresholds_set")
        counted_dve = sem("counted_dve")
        counted_act = sem("counted_act")
        totals_done = sem("totals_done")
        round_step = sem("round_step")
        rows_counted = sem("rows_counted")
        offsets_done = sem("offsets_done")
        place_done = sem("place_done")
        place_turned = sem("place_turned")
        split_step = sem("split_step")
        hot_step = sem("hot_step")
        hot_done = sem("hot_done")
        idx_ps = sem("idx_ps")
        idx_step = sem("idx_step")
        carried = sem("carried")
        idx_done = sem("idx_done")
        idx_kept = sem("idx_kept")
        taken_in = [sem(f"taken_in{k}") for k in range(2)]
        taken_turned = sem("taken_turned")
        takenT_done = sem("takenT_done")
        hidden_ps = sem("hidden_ps")
        hidden_done = sem("hidden_done")
        weight_step = sem("weight_step")
        weight_done = sem("weight_done")
        y_ps = sem("y_ps")
        y_step = sem("y_step")
        y_done = sem("y_done")
        added = [sem(f"added{k}") for k in range(2)]
        weights_in = [sem(f"weights_in{k}") for k in range(2)]

        block = ctx.enter_context(nc.Block())

        def all_experts(eng, step):
            step(item(0), False)
            step(item(1), False)
            with eng.Fori(1, E // 2 - 1) as i:
                step(Item(i * 2, i, 0), False)
                step(Item(i * 2 + 1, i, 1), False)
            step(item(E - 2), True)
            step(item(E - 1), True)

        @block.sync
        def _(sp):
            def load(it):
                if not early(it, 2):
                    sp.wait_ge(y_done, 2 * (it.no - 1))
                for dst, src in ((w1_sb, w1), (w2_sb, w2), (b1_sb, b1), (b2_sb, b2)):
                    a = src[bass.ds(it.no, 1)]
                    if src is w1:
                        a = a.rearrange("a d f -> (a d) f")
                    elif src is w2:
                        a = a.rearrange("a (p t) d -> (a p) t d", t=FT)
                    elif src is b1:
                        a = a.rearrange("a (p t) -> (a p) t", t=FT)
                    else:
                        a = a.broadcast_to([128, D])
                    sp.dma_start(dst[it.slot][tuple(slice(None) for _ in a.shape)], a).then_inc(weights_in[it.slot], 16)

            load(item(0))
            load(item(1))
            with sp.Fori(1, E // 2) as i:
                load(Item(i * 2, i, 0))
                load(Item(i * 2 + 1, i, 1))

        @block.tensor
        def _(pe):
            for c in range(NC):
                m = pe.transpose(banks[c // HALF][:, chunk(c % HALF)], logits[:, c, :], ident[0:C, 0:C])
                if c % HALF == HALF - 1:
                    m.then_inc(turned, 1)
            pe.wait_ge(dve_step, 2)
            for k in range(2):
                m = pe.transpose(banks[2][0:1, k * 128:(k + 1) * 128], row_ends[:, k:k + 1], ident)
            m.then_inc(ends_turned, 1)
            pe.wait_ge(ends_done, 2)
            pe.matmul(banks[3][:, 0:2 * E], const("ones")[0:1, :], ends[:, :, :].rearrange("p k e -> p (k e)"),
                      start=True, stop=True).then_inc(ends_spread, 1)
            pe.wait_ge(exp_sums_done, 1)
            pe.matmul(banks[4][:, 0:E], const("ones"), exp_sums[:, :], start=True, stop=True).then_inc(sums_spread, 1)
            with pe.Fori(0, ROUNDS) as r:
                pe.wait_ge(counted_dve, r * 2 + 2)
                pe.wait_ge(counted_act, r + 1)
                pe.matmul(banks[5][:, 0:3], const("same_expert"), counts[:, :], start=True,
                          stop=True).then_inc(totals_done, 1)
            pe.wait_ge(rows_counted, 1)
            pe.matmul(banks[6][:, 0:2], const("earlier_row"), row_counts[:, :], start=True, stop=True)
            pe.matmul(banks[6][:, 2:3], const("same_expert"), row_counts[:, 0:1], start=True,
                      stop=True).then_inc(offsets_done, 1)
            pe.wait_ge(place_done, 1)
            for c in range(NC):
                m = pe.transpose(banks[c // 4][0:C, (c % 4) * 128:(c % 4 + 1) * 128], place[:, chunk(c)], ident)
                if c in (3, NC - 1):
                    m.then_inc(place_turned, 1)

            def index(it):
                pe.wait_ge(hot_done, it.no + 1)
                pe.wait_ge(idx_done, it.no)
                for t in range(TILES):
                    m = pe.matmul(ps_idx[:, 0:2 * G], slot_hot[it.slot][:, t // RUN, :, t % RUN],
                                  block_val[it.slot][:, t // RUN, :, t % RUN],
                                  start=(t == 0), stop=(t == TILES - 1))
                m.then_inc(idx_ps, 1)

            pe.wait_ge(split_step, 2)
            index(item(0))

            def step(it, last):
                if not (last and it.slot == 1):
                    index(Item(it.no + 1, it.pair + it.slot, 1 - it.slot))
                pe.wait_ge(taken_in[it.slot], it.pair * 128 + 128)
                for k in range(2):
                    pe.wait_ge(takenT_done, it.no * 2)
                    for g in range(4):
                        m = pe.transpose(ps_T[k][:, g * 128:(g + 1) * 128], taken[it.slot][:, 4 * k + g, 0:D], ident)
                    m.then_inc(taken_turned, 1)
                pe.wait_ge(weights_in[it.slot], it.pair * 64 + 64)
                u = 0
                for k in range(2):
                    pe.wait_ge(takenT_done, it.no * 2 + k + 1)
                    for f in range(FT):
                        if u < 3:
                            pe.wait_ge(hidden_done, it.no * 8)
                        else:
                            pe.wait_ge(hidden_done, it.no * 8 + u - 2)
                        pe.matmul(ps_H[u % 3][:, :], w1_sb[it.slot][:, f * 128:(f + 1) * 128],
                                  takenT[:, k * 512:(k + 1) * 512], start=True, stop=True).then_inc(hidden_ps, 1)
                        u += 1
                for g in range(G):
                    if g % 4 == 0:
                        pe.wait_ge(hidden_done, it.no * 8 + 4 + g)
                        pe.wait_ge(y_done, it.no * 2)
                    for f in range(FT):
                        m = pe.matmul(ps_Y[g // 4][:, (g % 4) * D:(g % 4 + 1) * D],
                                      hidden[:, f, g * 128:(g + 1) * 128], w2_sb[it.slot][:, f, :],
                                      start=(f == 0), stop=(f == FT - 1), skip_group_check=True)
                    if g % 4 == 3:
                        m.then_inc(y_ps, 1)

            all_experts(pe, step)

        @block.scalar
        def _(act):
            act.wait_ge(top_done, 1)
            act.activation(scratch_act[:, :], lg_rows[:, :], ACT.Exp, bias=neg_top[:, 0:1],
                           accum_out=exp_sum[:, :]).then_inc(exp_done, 1)
            act.wait_ge(exp_done, 1)
            with act.Fori(0, ROUNDS) as r:
                act.wait_ge(thresholds_set, r + 1)
                act.activation(scratch_act[:, :], lg_rows[:, :], ACT.Sign, bias=thresholds[:, 2:3], scale=-1.0,
                               accum_out=counts[:, 2:3]).then_inc(counted_act, 1)
                act.wait_ge(counted_act, r + 1)

            def weights_of(it):
                act.wait_ge(taken_in[it.slot], it.pair * 128 + 128)
                act.wait_ge(weight_done, it.no)
                act.activation(weight_exp[:, :], taken[it.slot][:, :, bass.ds(it.no + D, 1)].rearrange("p g a -> p (g a)"),
                               ACT.Exp, bias=neg_top[:, bass.ds(it.no + 1, 1)]).then_inc(weight_step, 1)

            weights_of(item(0))

            def step(it, last):
                for k in range(2):
                    act.wait_ge(taken_turned, it.no * 2 + k + 1)
                    act.wait_ge(hidden_ps, it.no * 8)
                    act.copy(takenT[:, k * 512:(k + 1) * 512], ps_T[k][:, :]).then_inc(takenT_done, 1)
                act.wait_ge(weights_in[it.slot], it.pair * 64 + 64)
                act.wait_ge(y_ps, it.no * 2)
                for u in range(2 * FT):
                    act.wait_ge(hidden_ps, it.no * 8 + u + 1)
                    k, f = u // FT, u % FT
                    act.activation(hidden[:, f, k * 512:(k + 1) * 512], ps_H[u % 3][:, :], ACT.Gelu,
                                   bias=b1_sb[it.slot][:, f:f + 1]).then_inc(hidden_done, 1)
                if not (last and it.slot == 1):
                    weights_of(Item(it.no + 1, it.pair + it.slot, 1 - it.slot))

            all_experts(act, step)

        @block.gpsimd
        def _(pool):
            last_token = pool.to_reg(N - 1)

            def carry_waits(count):
                pool.wait_ge(carried, count)
                pool.tensor_tensor(carrier[:, :], const("ones")[0:1, 0:1], const("ones")[0:1, 0:1],
                                   ALU.mult).then_inc(carried, 1)

            def take(it):
                pool.wait_ge(idx_done, it.no + 1)
                if not early(it, 2):
                    pool.wait_ge(taken_turned, it.no * 2 - 2)
                    pool.wait_ge(weight_step, it.no - 1)
                carry_waits(0 if early(it, 1) else it.no * 3 - 2)
                for g in range(G):
                    pool.indirect_dma_start(
                        out=taken[it.slot][:, g, :], out_offset=None, in_=rows_dram[:, :],
                        in_offset=bass.IndirectOffsetOnAxis(ap=idx[it.slot][:, g:g + 1], axis=0),
                        bounds_check=last_token, oob_is_err=False).then_inc(taken_in[it.slot], 16)

            take(item(0))

            def step(it, last):
                if not (last and it.slot == 1):
                    after = Item(it.no + 1, it.pair + it.slot, 1 - it.slot)
                    take(after)
                for k in range(2):
                    pool.wait_ge(y_done, it.no * 2 + k + 1)
                    if k == 0:
                        pool.wait_ge(added[1 - it.slot], (it.pair + it.slot) * 128)
                    carry_waits(it.no * 3 + k + (1 if last and it.slot == 1 else 2))
                    for g in range(4 * k, 4 * k + 4):
                        pool.indirect_dma_start(
                            out=out_rows[:, :], out_offset=bass.IndirectOffsetOnAxis(ap=idx_add[it.slot][:, g:g + 1], axis=0),
                            in_=y[it.slot][:, g, :], in_offset=None, bounds_check=last_token, oob_is_err=True,
                            compute_op=ALU.add).then_inc(added[it.slot], 16)

            all_experts(pool, step)
            for k in range(2):
                pool.wait_ge(added[k], E // 2 * 128)

        @block.vector
        def _(dve):
            dve.tensor_copy(numbers16[:, :], const("numbers"))
            for k in range(2):
                dve.wait_ge(turned, k + 1)
                dve.tensor_copy(lg_rows[:, k * HALF * C:(k + 1) * HALF * C], banks[k][:, 0:HALF * C]
                                ).then_inc(lg_copied, 1)
            dve.wait_ge(lg_copied, 2)
            dve.tensor_reduce(row_ends[:, 0:1], lg_rows[:, :], AX_X, ALU.max).then_inc(dve_step, 1)
            dve.tensor_reduce(row_ends[:, 1:2], lg_rows[:, :], AX_X, ALU.min).then_inc(dve_step, 1)
            dve.wait_ge(ends_turned, 1)
            for k, op in enumerate((ALU.max, ALU.min)):
                dve.tensor_reduce(ends[:, k, :], banks[2][0:1, k * 128:(k + 1) * 128].rearrange("p (b e) -> p e b", e=E),
                                  AX_X, op).then_inc(ends_done, 1)
            dve.wait_ge(ends_spread, 1)
            dve.tensor_copy(ends_all[:, :, :].rearrange("p k e -> p (k e)"), banks[3][:, 0:2 * E]).then_inc(dve_step, 1)
            dve.wait_ge(dve_step, 3)
            dve.tensor_tensor(ends_sel[:, :, :], ends_all[:, :, :],
                              const("expert_of").unsqueeze(1).broadcast_to([128, 2, E]), ALU.mult).then_inc(dve_step, 1)
            dve.tensor_scalar(neg_top[:, 1:1 + E], ends_all[:, 0, :], -1.0, None, ALU.mult)
            dve.wait_ge(dve_step, 4)
            dve.tensor_reduce(top_low[:, :], ends_sel[:, :, :], AX_X, ALU.add).then_inc(dve_step, 1)
            dve.wait_ge(dve_step, 5)
            dve.tensor_scalar(neg_top[:, 0:1], top_low[:, 0:1], -1.0, None, ALU.mult).then_inc(top_done, 1)
            dve.tensor_tensor(width[:, :], top_low[:, 0:1], top_low[:, 1:2], ALU.subtract).then_inc(dve_step, 1)
            dve.tensor_copy(low[:, :], top_low[:, 1:2])
            dve.wait_ge(dve_step, 6)
            dve.tensor_scalar(width[:, :], width[:, :], 0.25, None, ALU.mult).then_inc(dve_step, 1)
            dve.wait_ge(dve_step, 7)
            dve.scalar_tensor_tensor(thresholds[:, :], const("k_of"), width[:, 0:1], low[:, 0:1].broadcast_to([128, 3]),
                                     ALU.mult, ALU.add).then_inc(thresholds_set, 1)
            dve.wait_ge(exp_done, 1)
            dve.tensor_scalar(exp_sums[:, :], const("expert_of"), exp_sum[:, 0:1], None, ALU.mult).then_inc(exp_sums_done, 1)
            dve.wait_ge(sums_spread, 1)
            dve.reciprocal(inv_sum[:, :], banks[4][:, 0:E])
            with dve.Fori(0, ROUNDS) as r:
                dve.wait_ge(thresholds_set, r + 1)
                for k in range(2):
                    if k:
                        dve.wait_ge(counted_dve, r * 2 + 1)
                    dve.tensor_scalar(scratch[:, :], lg_rows[:, :], thresholds[:, k:k + 1], None, ALU.is_lt, ALU.add,
                                      accum_out=counts[:, k:k + 1]).then_inc(counted_dve, 1)
                dve.wait_ge(totals_done, r + 1)
                dve.tensor_tensor(passed[:, :], banks[5][:, 0:3], const("bound"), ALU.is_le).then_inc(round_step, 1)
                dve.wait_ge(round_step, r * 4 + 1)
                dve.tensor_reduce(n_passed[:, :], passed[:, :], AX_X, ALU.add).then_inc(round_step, 1)
                dve.wait_ge(round_step, r * 4 + 2)
                dve.scalar_tensor_tensor(low[:, :], n_passed[:, :], width[:, 0:1], low[:, :], ALU.mult,
                                         ALU.add).then_inc(round_step, 1)
                dve.wait_ge(round_step, r * 4 + 3)
                dve.tensor_scalar(width[:, :], width[:, :], 0.25, None, ALU.mult).then_inc(round_step, 1)
                dve.wait_ge(round_step, r * 4 + 4)
                dve.scalar_tensor_tensor(thresholds[:, :], const("k_of"), width[:, 0:1],
                                         low[:, 0:1].broadcast_to([128, 3]), ALU.mult, ALU.add).then_inc(thresholds_set, 1)
            dve.scalar_tensor_tensor(high[:, :], width[:, :], 4.0, low[:, :], ALU.mult, ALU.add).then_inc(dve_step, 1)
            dve.wait_ge(dve_step, 8)
            dve.tensor_scalar(sure[:, :], lg_rows[:, :], high[:, 0:1], None, ALU.is_gt, ALU.add,
                              accum_out=row_counts[:, 0:1]).then_inc(dve_step, 1)
            dve.wait_ge(dve_step, 9)
            dve.scalar_tensor_tensor(band[:, :], lg_rows[:, :], low[:, 0:1], sure[:, :], ALU.is_ge,
                                     ALU.subtract).then_inc(dve_step, 1)
            dve.wait_ge(dve_step, 10)
            dve.tensor_reduce(row_counts[:, 1:2], band[:, :], AX_X, ALU.add).then_inc(rows_counted, 1)
            dve.wait_ge(offsets_done, 1)
            dve.tensor_copy(offsets[:, :], banks[6][:, 0:3]).then_inc(dve_step, 1)
            dve.wait_ge(dve_step, 11)
            dve.tensor_tensor(offsets[:, 1:2], offsets[:, 1:2], offsets[:, 2:3], ALU.add).then_inc(dve_step, 1)
            dve.wait_ge(dve_step, 12)
            ones = const("ones")[:, 0:1].broadcast_to([128, T])
            dve.tensor_tensor_scan(sure_rank[:, :], ones, sure[:, :], offsets[:, 0:1], ALU.mult, ALU.add)
            dve.tensor_tensor_scan(band_rank[:, :], ones, band[:, :], offsets[:, 1:2], ALU.mult,
                                   ALU.add).then_inc(dve_step, 1)
            dve.wait_ge(dve_step, 13)
            dve.tensor_tensor(sure_rank[:, :], sure_rank[:, :], sure[:, :], ALU.mult)
            dve.tensor_tensor(band_rank[:, :], band_rank[:, :], band[:, :], ALU.mult).then_inc(dve_step, 1)
            dve.wait_ge(dve_step, 14)
            dve.scalar_tensor_tensor(place[:, :], sure_rank[:, :], -1.0, band_rank[:, :], ALU.add,
                                     ALU.add).then_inc(place_done, 1)
            for k, (lo, hi) in enumerate(((0, 4), (4, NC))):
                dve.wait_ge(place_turned, k + 1)
                dve.tensor_copy(place_tok[:, :, lo * B:hi * B].rearrange("p e (c b) -> p c b e", b=B),
                                banks[k][0:C, 0:(hi - lo) * 128].rearrange("p (c b e) -> p c b e", b=B, e=E)
                                ).then_inc(split_step, 1)
            dve.wait_ge(split_step, 2)
            dve.tensor_scalar(place_int[:, :, :], place_tok[:, :, :], 7, None, ALU.arith_shift_right).then_inc(split_step, 1)
            dve.wait_ge(split_step, 3)
            dve.tensor_copy(block16[:, :, :], place_int[:, :, :]).then_inc(split_step, 1)
            dve.wait_ge(split_step, 4)
            dve.tensor_scalar(place_int[:, :, :], place_tok[:, :, :], 127, None, ALU.bitwise_and).then_inc(split_step, 1)
            dve.wait_ge(split_step, 5)
            dve.tensor_copy(slot16[:, :, :], place_int[:, :, :]).then_inc(split_step, 1)
            dve.wait_ge(split_step, 6)
            at = 128 * RUN
            slot_nos = numbers16[0:C, 0:at].rearrange("p (s t) -> p s t", t=RUN).unsqueeze(1)
            block_nos = numbers16[0:C, at:at + G * RUN].rearrange("p (s t) -> p s t", t=RUN).unsqueeze(1)
            at += G * RUN
            tile_nos = numbers16[0:C, at:at + TILES].rearrange("p (u t) -> p u t", t=RUN).unsqueeze(2)

            def hot(it):
                if not early(it, 2):
                    dve.wait_ge(idx_ps, it.no - 1)
                mine = bass.ds(it.no, 1)
                slots = slot16[:, mine, :].rearrange("p a (u t) -> p (a u) t", t=RUN).unsqueeze(2)
                blocks = block16[:, mine, :].rearrange("p a (u t) -> p (a u) t", t=RUN).unsqueeze(2)
                dve.tensor_tensor(slot_hot[it.slot][:, :, :, :], slot_nos.broadcast_to([C, RUNS, 128, RUN]),
                                  slots.broadcast_to([C, RUNS, 128, RUN]), ALU.is_equal)
                dve.wait_ge(hot_done, it.no)
                dve.tensor_tensor(block_hot[:, :, :, :], block_nos.broadcast_to([C, RUNS, G, RUN]),
                                  blocks.broadcast_to([C, RUNS, G, RUN]), ALU.is_equal).then_inc(hot_step, 1)
                dve.wait_ge(hot_step, it.no + 1)
                dve.tensor_scalar(block_val[it.slot][:, :, 0:G, :], block_hot[:, :, :, :], const("partition", C), None,
                                  ALU.mult)
                dve.tensor_tensor(block_val[it.slot][:, :, G:2 * G, :], block_hot[:, :, :, :],
                                  tile_nos.broadcast_to([C, RUNS, G, RUN]), ALU.mult).then_inc(hot_done, 1)

            def list_out(it):
                dve.wait_ge(idx_ps, it.no + 1)
                dve.tensor_scalar(idx_tile[:, :], ps_idx[:, G:2 * G], float(C), None, ALU.mult).then_inc(idx_step, 1)
                if not early(it, 2):
                    dve.wait_ge(taken_in[it.slot], it.pair * 128)
                    dve.wait_ge(idx_kept, it.no - 1)
                dve.wait_ge(idx_step, it.no + 1)
                dve.tensor_tensor(idx[it.slot][:, :], idx_tile[:, :], ps_idx[:, 0:G], ALU.add).then_inc(idx_done, 1)

            hot(item(0))
            list_out(item(0))
            hot(item(1))

            def step(it, last):
                if not (last and it.slot == 1):
                    after = Item(it.no + 1, it.pair + it.slot, 1 - it.slot)
                    list_out(after)
                if not last:
                    hot(Item(it.no + 2, it.pair + 1, it.slot))
                dve.wait_ge(y_done, it.no * 2)
                dve.wait_ge(weight_step, it.no + 1)
                dve.tensor_scalar(weight[:, :], weight_exp[:, :], inv_sum[:, bass.ds(it.no, 1)], None,
                                  ALU.mult).then_inc(weight_done, 1)
                if not early(it, 2):
                    dve.wait_ge(added[it.slot], it.pair * 128)
                dve.wait_ge(idx_done, it.no + 1)
                dve.tensor_copy(idx_add[it.slot][:, :], idx[it.slot][:, :]).then_inc(idx_kept, 1)
                for k in range(2):
                    dve.wait_ge(y_ps, it.no * 2 + k + 1)
                    dve.tensor_tensor(y_sum[:, 4 * k:4 * k + 4, :], ps_Y[k][:, :].rearrange("p (g d) -> p g d", d=D),
                                      b2_sb[it.slot][:, :].unsqueeze(1).broadcast_to([128, 4, D]), ALU.add
                                      ).then_inc(y_step, 1)
                    dve.wait_ge(y_step, it.no * 2 + k + 1)
                    dve.tensor_tensor(y[it.slot][:, 4 * k:4 * k + 4, :], y_sum[:, 4 * k:4 * k + 4, :],
                                      weight[:, 4 * k:4 * k + 4].unsqueeze(2).broadcast_to([128, 4, D]), ALU.mult
                                      ).then_inc(y_done, 1)

            all_experts(dve, step)


_INS = ["x", "L0_tok_W_ve", "L0_tok_b_ve", "L0_tok_W_lin", "L0_tok_b_lin", "L0_attn_wq", "L0_attn_bq", "L0_attn_wk",
        "L0_attn_bk", "L0_attn_wv", "L0_attn_bv", "L0_attn_wg", "L0_attn_bg", "L0_ffn_Wr", "L0_ffn_W1", "L0_ffn_b1",
        "L0_ffn_W2", "L0_ffn_b2"]


def kernel(**inputs):
    import concourse.bacc as bacc
    from concourse.bass_utils import run_bass_kernel_spmd

    nc = bacc.Bacc("TRN2", target_bir_lowering=False, num_devices=1)
    data = {name: np.ascontiguousarray(inputs[name]) for name in _INS}
    data["L0_ffn_W1"] = np.ascontiguousarray(
        data["L0_ffn_W1"].reshape(E, D, 128, FT).transpose(0, 1, 3, 2).reshape(E, D, F))
    data["consts"] = constants()
    arrays, args = {}, []
    for name, a in data.items():
        arrays[f"in_{name}"] = a
        args.append(nc.dram_tensor(f"in_{name}", a.shape, mybir.dt.from_np(a.dtype), kind="ExternalInput").ap())
    args.append(nc.dram_tensor("out", (B, T, D), F32, kind="ExternalOutput").ap())
    program(nc, *args)
    r = run_bass_kernel_spmd(nc, [arrays], core_ids=[0])
    return r.results[0]["out"]
```

```python
from contextlib import ExitStack

import numpy as np

import concourse.bass as bass
from concourse import mybir

F32 = mybir.dt.float32
BF16 = mybir.dt.bfloat16
I32 = mybir.dt.int32
U32 = mybir.dt.uint32
ALU = mybir.AluOpType
ACT = mybir.ActivationFunctionType
AX_X = mybir.AxisListType.X

B, CH, T, D = 16, 32, 750, 128
H, DH = 8, 16
C = 125
NC = T // C
HALF = NC // 2
N = B * T
E, F, CAP = 8, 512, 1024
FT = F // 128
G = CAP // 128
TILES = N // C
RUN = 4
RUNS = TILES // RUN
ROW = D + E
ALPHA = 0.1
EPS = 1e-5
ROUNDS = 16
DVE_PART = 500
UNROLL = 4


class Item:

    def __init__(self, no, pair, slot):
        self.no, self.pair, self.slot = no, pair, slot


def item(no):
    return Item(no, no // 2, no % 2)


UNITS = ["x0", "x1", "o0", "o1", "q0", "a5", "q1", "k0", "k1", "a4", "g0", "g1", "h0", "a3",
         "t0", "t1", "v0", "v1", "v2", "a2", "h1", "b0", "b1", "s0", "a1", "s1", "lg", "a0"]
BANKS = 4
OF_ITEM = {"o": -1, "b": -1, "l": -1, "a": 0, "h": 2}


def bank_of(unit):
    return UNITS.index(unit) % BANKS


def before_in_bank(step, unit):
    at = UNITS.index(unit)
    while True:
        at -= BANKS
        if at < 0:
            at, step = at + len(UNITS), step - 1
        if isinstance(step, int) and step < -2:
            return None, None
        former = UNITS[at]
        no = step + OF_ITEM.get(former[0], 1)
        if not isinstance(no, int) or 0 <= no < B:
            return former, no


def early(it, n):
    return it is not None and isinstance(it.no, int) and it.no < n


CONSTS = {}


def constants():
    p = np.arange(128)
    head = p // DH
    gamma = 1.0 - 2.0 ** (-5.0 - head.astype(np.float64))
    i = np.arange(C)
    parts = {
        "ident": np.eye(128),
        "ones": np.ones((128, 128)),
        "keep": (p[:, None] >= i[None, :]),
        "q_decay": gamma[:, None] ** (-i[None, :]) / np.sqrt(DH),
        "k_decay": gamma[:, None] ** i[None, :],
        "chunk_decay": gamma[:, None] ** C,
        "odd_head": (head[:, None] % 2 == 1),
        "block_decay": (head[:, None] == head[None, :]) * gamma[:, None] ** C,
        "same_expert": (p[:, None] % E == p[None, :] % E),
        "earlier_row": (p[:, None] % E == p[None, :] % E) & (p[:, None] // E < p[None, :] // E),
        "expert_of": (p[:, None] % E == np.arange(E)[None, :]),
        "k_of": np.broadcast_to(np.arange(1, 4)[None, :], (128, 3)),
        "same_twice": 2.0 * (p[:, None] % E == p[None, :] % E),
        "sign_base": np.broadcast_to(np.array([0, T - DVE_PART, T])[None, :], (128, 3)),
        "partition": p[:, None],
        "even_odd": np.concatenate([np.broadcast_to(head % 2 == k, (128, 128)) for k in range(2)], axis=1),
        "half": np.full((128, NC), -0.5),
        "numbers": np.broadcast_to(np.concatenate([
            np.repeat(np.arange(128), RUN), np.repeat(np.arange(G), RUN),
            (np.arange(B)[None, :] * NC + np.arange(NC)[:, None]).reshape(-1)])[None, :],
            (128, (128 + G) * RUN + TILES)),
    }
    at = 0
    cols = []
    for name, a in parts.items():
        CONSTS[name] = (at, a.shape[1])
        at += a.shape[1]
        cols.append(a.astype(np.float32))
    return np.ascontiguousarray(np.concatenate(cols, axis=1))


def program(nc, x, w_ve, b_ve, w_lin, b_lin, wq, bq, wk, bk, wv, bv, wg, bg, wr, w1, b1, w2, b2,
            consts, out):
    constants()
    smooth_dram = nc.dram_tensor("smooth_dram", (B, CH, T), F32).ap()
    rows_dram = nc.dram_tensor("rows_dram", (N, ROW), F32).ap()
    out_rows = out.rearrange("b t d -> (b t) d")
    x_rows = x.rearrange("b c t -> (b c) t")
    smooth_rows = smooth_dram.rearrange("b c t -> (b c) t")
    out_items = out.rearrange("b (c p) d -> b p c d", p=C)
    row_items = rows_dram.rearrange("(b c p) d -> b p c d", c=NC, p=C)

    with ExitStack() as ctx:
        def sb(name, shape, dt=F32):
            return ctx.enter_context(nc.sbuf_tensor(name, shape, dt))

        def psum(name, shape, dt=F32):
            return ctx.enter_context(nc.psum_tensor(name, shape, dt))

        def sem(name):
            return ctx.enter_context(nc.semaphore(name))

        cst = sb("cst", [128, consts.shape[1]])
        numbers16 = sb("numbers16", [128, (128 + G) * RUN + TILES], BF16)

        def const(name, rows=128):
            at, n = CONSTS[name]
            return cst[0:rows, at:at + n]

        ident = const("ident")

        logits = sb("logits", [C, NC, B * E])
        w_col = sb("w_col", [128, 3])
        v_bias = sb("v_bias", [C, D])
        wr_wide = sb("wr_wide", [D, D])
        wT = sb("wT", [D, 4, D])
        emb_w = sb("emb_w", [CH + 1, D])
        weight_in = sb("weight_in", [D, 5, D])
        ve_in = sb("ve_in", [D, CH])
        bve_in = sb("bve_in", [D, 1])
        lin_T = sb("lin_T", [D, D])
        blin_in = sb("blin_in", [1, D])

        h2_sb = [sb(f"h2_sb{k}", [C, NC, D]) for k in range(2)]
        row_sb = [sb(f"row_sb{k}", [C, NC, ROW]) for k in range(2)]

        stage1 = ExitStack()

        def s1(name, shape, dt=F32):
            return stage1.enter_context(nc.sbuf_tensor(name, shape, dt))

        xin = s1("xin", [128, 4, T])
        diff = s1("diff", [128, T])
        scaled = s1("scaled", [128, T])
        fwd = s1("fwd", [128, T])
        bwd = s1("bwd", [128, T])
        smooth = s1("smooth", [128, 4, T])
        keep9 = s1("keep9", [128, T])
        s_in = [s1(f"s_in{k}", [CH + 1, T]) for k in range(2)]
        h_sb = [s1(f"h_sb{k}", [C, NC, D]) for k in range(2)]
        h_kept = s1("h_kept", [C, NC, D])
        stats = s1("stats", [C, NC, 6])
        moments = s1("moments", [C, NC, 2])
        rstd = s1("rstd", [C, NC])
        xn = s1("xn", [C, NC, D])
        xT = [s1(f"xT{k}", [D, T]) for k in range(2)]
        q_dec = [s1(f"q_dec{k}", [D, T]) for k in range(2)]
        q_odd = [s1(f"q_odd{k}", [D, T]) for k in range(2)]
        k_dec = [s1(f"k_dec{k}", [D, T]) for k in range(2)]
        k_tok = [s1(f"k_tok{k}", [C, NC, D]) for k in range(2)]
        v_split = [s1(f"v_split{k}", [C, NC, 2, D]) for k in range(2)]
        v_tok = [s1(f"v_tok{k}", [C, NC, D]) for k in range(2)]
        gate = [s1(f"gate{k}", [D, T]) for k in range(2)]
        prob = [s1(f"prob{k}", [C, H, C]) for k in range(2)]
        attn = s1("attn", [D, T])
        state = [s1(f"state{k}", [D, NC - 1, D]) for k in range(2)]
        stats2 = s1("stats2", [C, NC, 6])
        moments2 = s1("moments2", [C, NC, 2])
        rstd2 = s1("rstd2", [C, NC])
        x2T = s1("x2T", [D, T])

        def p1(name, shape):
            return stage1.enter_context(nc.psum_tensor(name, shape, F32))

        bank = [p1(f"bank{k}", [128, 512]) for k in range(BANKS)]
        ps_score = p1("ps_score", [128, 4, 512])

        embedding_in = sem("embedding_in")
        consts_in = sem("consts_in")
        x_in = [sem(f"x_in{k}") for k in range(4)]
        scan_step = sem("scan_step")
        smooth_done = sem("smooth_done")
        smooth_out = sem("smooth_out")
        setup_pe = sem("setup_pe")
        setup_act = sem("setup_act")
        ones_set = sem("ones_set")
        s_loaded = [sem(f"s_loaded{k}") for k in range(2)]
        filled = {u: sem(f"filled_{u}") for u in UNITS}
        read = {u: sem(f"read_{u}") for u in UNITS}
        stats_done = sem("stats_done")
        moments_step = sem("moments_step")
        rstd_done = sem("rstd_done")
        xn_done = sem("xn_done")
        q_odd_done = sem("q_odd_done")
        low_scored = sem("low_scored")
        high_scored = sem("high_scored")
        low_masked = sem("low_masked")
        high_copied = sem("high_copied")
        high_masked = sem("high_masked")
        state_step = sem("state_step")
        state_done = sem("state_done")
        stats2_done = sem("stats2_done")
        moments2_step = sem("moments2_step")
        rstd2_done = sem("rstd2_done")
        xn2_done = sem("xn2_done")
        logits_done = sem("logits_done")
        v_split_done = sem("v_split_done")
        h_moved = sem("h_moved")
        h2_out = [sem(f"h2_out{k}") for k in range(2)]
        rows_out = [sem(f"rows_out{k}") for k in range(2)]
        stage1_block = nc.Block()
        stage1.enter_context(stage1_block)
        block = stage1_block

        def chunk(c):
            return slice(c * C, (c + 1) * C)

        def items_of_loop(i, odd):
            if odd:
                return (i * 2 + 1, Item(i * 2, i, 0), Item(i * 2 + 1, i, 1), Item(i * 2 + 2, i + 1, 0),
                        Item(i * 2 + 3, i + 1, 1))
            return (i * 2, Item(i * 2 - 1, i - 1, 1), Item(i * 2, i, 0), Item(i * 2 + 1, i, 1),
                    Item(i * 2 + 2, i + 1, 0))

        def all_steps(eng, step):
            def single(n):
                step(n, *(item(k) if 0 <= k < B else None for k in range(n - 1, n + 3)))

            for n in range(-2, 4):
                single(n)
            with eng.Fori(2, B // 2 - 1) as i:
                for odd in range(2):
                    step(*items_of_loop(i, odd))
            for n in range(B - 2, B + 1):
                single(n)

        def prob_free(eng, own, c):
            if c < NC - 2:
                eng.wait_ge(filled[f"a{c + 2}"], own.no + 1)
            elif not early(own, 1):
                eng.wait_ge(filled[f"a{c + 2 - NC}"], own.no)

        @block.sync
        def _(sp):
            for dst, src in [
                    (weight_in[:, 4, :], w_lin), (cst[:, 0:256], consts[:, 0:256]), (ve_in[:, :], w_ve),
                    (bve_in[:, :], b_ve.unsqueeze(1)), (blin_in[:, :], b_lin.unsqueeze(0))]:
                sp.dma_start(dst, src).then_inc(embedding_in, 16)
            sp.dma_start(cst[:, 256:], consts[:, 256:]).then_inc(consts_in, 16)
            for dst, src in [
                    (weight_in[:, 0, :], wq), (weight_in[:, 1, :], wk), (weight_in[:, 2, :], wv),
                    (weight_in[:, 3, :], wg), (w_col[:, 0:1], bq.unsqueeze(1)), (w_col[:, 1:2], bk.unsqueeze(1)),
                    (v_bias[:, :], bv.unsqueeze(0).broadcast_to([C, D])),
                    (w_col[:, 2:3], bg.unsqueeze(1)),
                    (wr_wide[:, 0:E], wr)]:
                sp.dma_start(dst, src).then_inc(consts_in, 16)
            def smooth_part(j):
                sp.wait_ge(smooth_done, j + 1)
                sp.dma_start(smooth_rows[j * 128:(j + 1) * 128, :], smooth[:, j, :]).then_inc(smooth_out, 16)

            smooth_part(0)

            def step(n, before, own, after, coming):
                if coming:
                    if early(coming, 1):
                        sp.wait_ge(smooth_out, 16)
                    elif early(coming, 5) and not early(coming, 4):
                        sp.wait_ge(smooth_out, 64)
                    if not early(coming, 2):
                        sp.wait_ge(filled["h1"], coming.no - 1)
                    sp.dma_start(s_in[coming.slot][0:CH, :],
                                 smooth_dram[bass.ds(coming.no, 1)].rearrange("a c t -> (a c) t")
                                 ).then_inc(s_loaded[coming.slot], 16)
                    if early(coming, 3):
                        smooth_part(coming.no + 1)
                if before:
                    sp.wait_ge(read["o1"], before.no + 1)
                    sp.dma_start(out_items[bass.ds(before.no, 1)].rearrange("a p c d -> (a p) c d"),
                                 h2_sb[before.slot][:, :, :]).then_inc(h2_out[before.slot], 16)
                    sp.wait_ge(xn2_done, before.no + 1)
                    sp.wait_ge(logits_done, before.no + 1)
                    sp.dma_start(row_items[bass.ds(before.no, 1)].rearrange("a p c d -> (a p) c d"),
                                 row_sb[before.slot][:, :, :]).then_inc(rows_out[before.slot], 16)

            all_steps(sp, step)

        @block.tensor
        def _(pe):
            pe.wait_ge(embedding_in, 16 * 5)
            pe.transpose(bank[0][:, 0:D], weight_in[:, 4, :], ident).then_inc(setup_pe, 1)
            pe.wait_ge(setup_act, 1)
            pe.matmul(bank[2][0:CH, 0:D], ve_in[:, :], lin_T[:, :], start=True, stop=True)
            pe.matmul(bank[2][CH:CH + 1, D:2 * D], bve_in[:, :], lin_T[:, :], start=True, stop=False,
                      skip_group_check=True)
            pe.matmul(bank[2][CH:CH + 1, D:2 * D], const("ones")[0:1, 0:1], blin_in[:, :], start=False, stop=True,
                      skip_group_check=True).then_inc(setup_pe, 1)
            pe.wait_ge(consts_in, 16 * 10)
            for k in range(4):
                t = pe.transpose(bank[1][:, k * D:(k + 1) * D], weight_in[:, k, :], ident)
            t.then_inc(setup_pe, 1)
            pe.wait_ge(setup_act, 4)

            def claim(step, unit):
                former, no = before_in_bank(step, unit)
                if former:
                    pe.wait_ge(read[former], no + 1)
                return bank[bank_of(unit)]

            def scores(own, c, last):
                done = own.no * NC + (NC - 1 - c)
                if c == NC - 1:
                    pe.wait_ge(read["q1"], own.no + 1)
                    pe.wait_ge(q_odd_done, own.no + 1)
                    pe.wait_ge(read["k1"], own.no + 1)
                pe.wait_ge(low_masked, done)
                pe.wait_ge(high_masked if last and c < NC - 1 else high_copied, done)
                for h in (0, 2, 4, 6, 1, 3, 5, 7):
                    g, lo = h // 2, 32 * (h // 2)
                    rows = slice(lo, lo + 32) if h % 2 else slice(lo, lo + DH)
                    q = (q_odd if h % 2 else q_dec)[own.slot]
                    at = (h % 2) * C
                    m = pe.matmul(ps_score[0:C, g, at:at + C], k_dec[own.slot][rows, chunk(c)], q[rows, chunk(c)],
                                  start=True, stop=True)
                    if h == 3:
                        m.then_inc(low_scored, 1)
                m.then_inc(high_scored, 1)

            def values(own, c):
                unit = f"a{c}"
                o = claim(own.no, unit)[:, 0:C]
                if c == NC - 1:
                    pe.wait_ge(state_done, own.no + 1)
                    pe.wait_ge(v_split_done, own.no * 2 + 2)
                else:
                    pe.matmul(o, state[own.slot][:, c, :], q_dec[own.slot][:, chunk(c)], start=True, stop=False,
                              skip_group_check=True)
                pe.wait_ge(low_masked, own.no * NC + (NC - c))
                pe.wait_ge(high_masked, own.no * NC + (NC - c))
                for k, h in enumerate((0, 2, 4, 6, 1, 3, 5, 7)):
                    rows = slice(h // 2 * 32, h // 2 * 32 + 32)
                    m = pe.matmul(o[rows, :], v_split[own.slot][:, c, h % 2, rows], prob[c % 2][:, h, :],
                                  start=(c == NC - 1 and k < 4), stop=(k >= 4), skip_group_check=True)
                m.then_inc(filled[unit], 1)

            def step(n, before, own, after, coming):
                def h_unit(k):
                    if early(coming, 1):
                        pe.wait_ge(ones_set, 1)
                    pe.wait_ge(s_loaded[coming.slot], coming.pair * 16 + 16)
                    ps = claim(n, f"h{k}")
                    for c in range(HALF):
                        m = pe.matmul(ps[0:C, c * D:(c + 1) * D], s_in[coming.slot][:, chunk(k * HALF + c)],
                                      emb_w[:, :], start=True, stop=True)
                    m.then_inc(filled[f"h{k}"], 1)

                def x_units():
                    pe.wait_ge(xn_done, after.no + 1)
                    for k in range(2):
                        ps = claim(n, f"x{k}")
                        for c in range(HALF):
                            m = pe.transpose(ps[:, chunk(c)], xn[:, k * HALF + c, :], ident[0:C, 0:C])
                        m.then_inc(filled[f"x{k}"], 1)

                def o_units():
                    for k in range(2):
                        pe.wait_ge(read["a0"], before.no + 1)
                        ps = claim(n, f"o{k}")
                        for c in range(HALF):
                            m = pe.transpose(ps[0:C, c * D:(c + 1) * D], attn[:, chunk(k * HALF + c)], ident)
                        m.then_inc(filled[f"o{k}"], 1)

                def project(name, w, ks=(0, 1)):
                    for k in ks:
                        ps = claim(n, f"{name}{k}")
                        pe.wait_ge(read[f"x{k}"], after.no + 1)
                        pe.matmul(ps[:, 0:HALF * C], wT[:, w, :], xT[after.slot][:, k * HALF * C:(k + 1) * HALF * C],
                                  start=True, stop=True).then_inc(filled[f"{name}{k}"], 1)

                def k_tok_units():
                    for k in range(2):
                        pe.wait_ge(read[f"k{k}"], after.no + 1)
                        ps = claim(n, f"t{k}")
                        for c in range(HALF):
                            m = pe.transpose(ps[0:C, c * D:(c + 1) * D], k_dec[after.slot][:, chunk(k * HALF + c)],
                                             ident)
                        m.then_inc(filled[f"t{k}"], 1)

                def v_units():
                    for k in range(3):
                        ps = claim(n, f"v{k}")
                        for c in range(2):
                            m = pe.matmul(ps[0:C, c * D:(c + 1) * D], xT[after.slot][:, chunk(2 * k + c)],
                                          wT[:, 2, :], start=True, stop=True)
                        m.then_inc(filled[f"v{k}"], 1)

                def state_unit(k):
                    pe.wait_ge(read["t1"], after.no + 1)
                    pe.wait_ge(read["v2"], after.no + 1)
                    ps = claim(n, f"s{k}")
                    cs = ([4, 3, 2, 1], [0])[k]
                    for c in cs:
                        at = (c - cs[-1]) * D
                        m = pe.matmul(ps[:, at:at + D], k_tok[after.slot][:, c + 1, :],
                                      v_tok[after.slot][:, c + 1, :], start=True, stop=True)
                    m.then_inc(filled[f"s{k}"], 1)

                def b_units():
                    pe.wait_ge(xn2_done, before.no + 1)
                    for k in range(2):
                        ps = claim(n, f"b{k}")
                        for c in range(HALF):
                            m = pe.transpose(ps[:, chunk(c)], row_sb[before.slot][:, k * HALF + c, 0:D],
                                             ident[0:C, 0:C])
                        m.then_inc(filled[f"b{k}"], 1)

                def logits_unit():
                    pe.wait_ge(read["b1"], before.no + 1)
                    ps = claim(n, "lg")
                    for c in range(NC):
                        m = pe.matmul(ps[0:C, c * E:c * E + D], x2T[:, chunk(c)], wr_wide[:, :], start=True, stop=True)
                    m.then_inc(filled["lg"], 1)

                if own:
                    scores(own, 5, after is None)
                if after:
                    x_units()
                if before:
                    o_units()
                if after:
                    project("q", 0, (0,))
                if own:
                    scores(own, 4, after is None)
                    values(own, 5)
                if after:
                    project("q", 0, (1,))
                    project("k", 1)
                if own:
                    scores(own, 3, after is None)
                    values(own, 4)
                if after:
                    project("g", 3)
                if coming:
                    h_unit(0)
                if own:
                    scores(own, 2, after is None)
                    values(own, 3)
                if after:
                    k_tok_units()
                    v_units()
                if own:
                    scores(own, 1, after is None)
                    values(own, 2)
                if coming:
                    h_unit(1)
                if before:
                    b_units()
                if after:
                    state_unit(0)
                if own:
                    scores(own, 0, after is None)
                    values(own, 1)
                if after:
                    state_unit(1)
                if before:
                    logits_unit()
                if own:
                    values(own, 0)

            all_steps(pe, step)

        @block.scalar
        def _(act):
            act.dma_start(xin[:, 0, :], x_rows[0:128, :]).then_inc(x_in[0], 16)
            for j in range(1, 4):
                act.dma_start(xin[:, j, :], x_rows[j * 128:(j + 1) * 128, :]).then_inc(x_in[j], 16)
            act.wait_ge(setup_pe, 1)
            act.copy(lin_T[:, :], bank[0][:, 0:D]).then_inc(setup_act, 1)
            act.wait_ge(setup_pe, 2)
            act.copy(emb_w[0:CH, :], bank[2][0:CH, 0:D]).then_inc(setup_act, 1)
            act.copy(emb_w[CH:CH + 1, :], bank[2][CH:CH + 1, D:2 * D]).then_inc(setup_act, 1)
            act.wait_ge(setup_pe, 3)
            act.copy(wT[:, :, :].rearrange("p k d -> p (k d)"), bank[1][:, :]).then_inc(setup_act, 1)

            def step(n, before, own, after, coming):
                def copy_out(it, unit, dst, rows, cols):
                    act.wait_ge(filled[unit], it.no + 1)
                    act.copy(dst, bank[bank_of(unit)][0:rows, 0:cols]).then_inc(read[unit], 1)

                def copy_h(k):
                    copy_out(coming, f"h{k}", h_sb[coming.slot][:, k * HALF:(k + 1) * HALF, :].rearrange("p c d -> p (c d)"),
                             C, HALF * D)

                def high_scores(c):
                    if not after:
                        return
                    act.wait_ge(high_scored, own.no * NC + (NC - c))
                    prob_free(act, own, c)
                    act.copy(prob[c % 2][:, H // 2:H, :].rearrange("p (g e) i -> p g (e i)", e=2),
                             ps_score[0:C, 2:4, 0:2 * C]).then_inc(high_copied, 1)

                if own:
                    high_scores(5)
                if after:
                    if not early(after, 2):
                        act.wait_ge(filled["v2"], after.no - 1)
                    for k in range(2):
                        copy_out(after, f"x{k}", xT[after.slot][:, k * HALF * C:(k + 1) * HALF * C], D, HALF * C)
                if own:
                    high_scores(4)
                    if not early(own, 1):
                        act.wait_ge(read["o1"], own.no)
                    act.copy(h_kept[:, :, :], h_sb[own.slot][:, :, :]).then_inc(h_moved, 1)
                    high_scores(3)
                if after:
                    if not early(after, 2):
                        act.wait_ge(read["a0"], after.no - 1)
                    for k in range(2):
                        act.wait_ge(filled[f"g{k}"], after.no + 1)
                        act.activation(gate[after.slot][:, k * HALF * C:(k + 1) * HALF * C],
                                       bank[bank_of(f"g{k}")][:, 0:HALF * C], ACT.Silu,
                                       bias=w_col[:, 2:3]).then_inc(read[f"g{k}"], 1)
                if coming:
                    if not early(coming, 2):
                        act.wait_ge(h_moved, coming.no - 1)
                        act.wait_ge(xn_done, coming.no - 1)
                    copy_h(0)
                if own:
                    high_scores(2)
                if after:
                    for k in range(2):
                        copy_out(after, f"t{k}", k_tok[after.slot][:, k * HALF:(k + 1) * HALF, :].rearrange("p c d -> p (c d)"),
                                 C, HALF * D)
                if own:
                    high_scores(1)
                if coming:
                    copy_h(1)
                if before:
                    if not early(before, 1):
                        act.wait_ge(filled["lg"], before.no)
                    for k in range(2):
                        copy_out(before, f"b{k}", x2T[:, k * HALF * C:(k + 1) * HALF * C], D, HALF * C)
                if own:
                    high_scores(0)

            all_steps(act, step)

        @block.gpsimd
        def _(pool):
            pool.memset(s_in[0][CH:CH + 1, :], 1.0)
            pool.memset(s_in[1][CH:CH + 1, :], 1.0).then_inc(ones_set, 1)
            pool.wait_ge(consts_in, 16 * 10)

            def step(n, before, own, after, coming):
                def high_mask(c):
                    if not after:
                        return
                    done = own.no * NC + (NC - 1 - c)
                    pool.wait_ge(high_copied, done + 1)
                    p = prob[c % 2][:, H // 2:H, :]
                    pool.tensor_tensor(p, p, const("keep", C).unsqueeze(1).broadcast_to([C, H // 2, C]),
                                       ALU.mult).then_inc(high_masked, 1)

                def inverse_root(moments_ready, done, m, r):
                    pool.wait_ge(moments_ready, done)
                    return pool.tensor_tensor(r[:, :], m[:, :, 1], const("half", C), ALU.pow)

                def split_values(k):
                    if k == 0:
                        pool.wait_ge(read["v2"], after.no + 1)
                        if not early(after, 2):
                            pool.wait_ge(filled["a0"], after.no - 1)
                    cs = slice(k * HALF, (k + 1) * HALF)
                    pool.tensor_tensor(v_split[after.slot][:, cs, :, :],
                                       v_tok[after.slot][:, cs, :].unsqueeze(2).broadcast_to([C, HALF, 2, D]),
                                       const("even_odd", C).rearrange("p (w d) -> p w d", w=2).unsqueeze(1)
                                       .broadcast_to([C, HALF, 2, D]), ALU.mult).then_inc(v_split_done, 1)

                if own:
                    high_mask(5)
                    high_mask(4)
                    high_mask(3)
                if before:
                    inverse_root(moments2_step, 2 * before.no + 2, moments2, rstd2).then_inc(rstd2_done, 1)
                if own:
                    high_mask(2)
                if after:
                    pool.wait_ge(read["q0"], after.no + 1)
                    pool.wait_ge(read["q1"], after.no + 1)
                    pool.tensor_tensor(q_odd[after.slot][:, :], q_dec[after.slot][:, :],
                                       const("odd_head").broadcast_to([D, T]), ALU.mult).then_inc(q_odd_done, 1)
                if own:
                    high_mask(1)
                if after:
                    split_values(0)
                if coming:
                    inverse_root(moments_step, 2 * coming.no + 2, moments, rstd).then_inc(rstd_done, 1)
                if own:
                    high_mask(0)
                if after:
                    split_values(1)

            all_steps(pool, step)

        @block.vector
        def _(dve):
            dve.memset(wr_wide[:, E:D], 0.0)
            dve.memset(keep9[:, :], 1.0 - ALPHA)
            dve.memset(diff[:, 0:1], 0.0).then_inc(scan_step, 1)

            def smooth_part(j):
                dve.wait_ge(x_in[j], 16)
                if j:
                    dve.wait_ge(smooth_done, j)
                dve.tensor_tensor(diff[:, 1:T], xin[:, j, 1:T], xin[:, j, 0:T - 1], ALU.subtract).then_inc(scan_step, 1)
                dve.wait_ge(scan_step, 5 * j + 2)
                dve.tensor_scalar(scaled[:, :], diff[:, :], 0.5 * ALPHA, None, ALU.mult).then_inc(scan_step, 1)
                dve.wait_ge(scan_step, 5 * j + 3)
                dve.tensor_tensor_scan(fwd[:, :], keep9[:, :], scaled[:, :], 0.0, ALU.mult, ALU.add).then_inc(scan_step, 1)
                dve.wait_ge(scan_step, 5 * j + 4)
                dve.tensor_scalar(scaled[:, T - 1:T], diff[:, T - 1:T], 0.5, None, ALU.mult).then_inc(scan_step, 1)
                dve.wait_ge(scan_step, 5 * j + 5)
                dve.tensor_tensor_scan(bwd[:, ::-1], keep9[:, :], scaled[:, ::-1], 0.0, ALU.mult,
                                       ALU.add).then_inc(scan_step, 1)
                dve.wait_ge(scan_step, 5 * j + 6)
                dve.tensor_tensor(smooth[:, j, :], fwd[:, :], bwd[:, :], ALU.add).then_inc(smooth_done, 1)

            smooth_part(0)
            smooth_part(1)

            def step(n, before, own, after, coming):
                def low_scores(c):
                    dve.wait_ge(low_scored, own.no * NC + (NC - c))
                    prob_free(dve, own, c)
                    keep = const("keep", C).unsqueeze(1).unsqueeze(1).broadcast_to([C, 2, 2, C])
                    dve.tensor_tensor(prob[c % 2][:, 0:H // 2, :].rearrange("p (g e) i -> p g e i", e=2),
                                      ps_score[0:C, 0:2, 0:2 * C].rearrange("p g (e i) -> p g e i", e=2),
                                      keep, ALU.mult).then_inc(low_masked, 1)
                    if not after:
                        dve.wait_ge(high_scored, own.no * NC + (NC - c))
                        dve.tensor_tensor(prob[c % 2][:, H // 2:H, :].rearrange("p (g e) i -> p g e i", e=2),
                                          ps_score[0:C, 2:4, 0:2 * C].rearrange("p g (e i) -> p g e i", e=2),
                                          keep, ALU.mult).then_inc(high_masked, 1)

                def state_products(k):
                    lo, hi = ((1, NC - 1), (0, 1))[k]
                    dve.wait_ge(filled[f"s{k}"], after.no + 1)
                    dve.tensor_tensor(state[after.slot][:, lo:hi, :],
                                      bank[bank_of(f"s{k}")][:, 0:(hi - lo) * D].rearrange("p (c d) -> p c d", d=D),
                                      const("block_decay").unsqueeze(1).broadcast_to([D, hi - lo, D]),
                                      ALU.mult).then_inc(read[f"s{k}"], 1)

                def states():
                    st = state[after.slot]
                    dve.wait_ge(read["s1"], after.no + 1)
                    for k, c in enumerate(range(NC - 3, -1, -1)):
                        if k:
                            dve.wait_ge(state_step, after.no * (NC - 3) + k)
                        i = dve.scalar_tensor_tensor(st[:, c, :], st[:, c + 1, :], const("chunk_decay"), st[:, c, :],
                                                     ALU.mult, ALU.add)
                        i.then_inc(state_done if c == 0 else state_step, 1)

                def gated_out(c):
                    if c == NC - 1:
                        dve.wait_ge(read["g1"], own.no + 1)
                        if not early(own, 1):
                            dve.wait_ge(filled["o1"], own.no)
                    dve.wait_ge(filled[f"a{c}"], own.no + 1)
                    dve.tensor_tensor(attn[:, chunk(c)], bank[bank_of(f"a{c}")][:, 0:C], gate[own.slot][:, chunk(c)],
                                      ALU.mult).then_inc(read[f"a{c}"], 1)

                def residual():
                    if not early(before, 2):
                        dve.wait_ge(h2_out[before.slot], before.pair * 16)
                    dve.wait_ge(h_moved, before.no + 1)
                    for k in range(2):
                        cs = slice(k * HALF, (k + 1) * HALF)
                        dve.wait_ge(filled[f"o{k}"], before.no + 1)
                        dve.tensor_tensor(h2_sb[before.slot][:, cs, :],
                                          bank[bank_of(f"o{k}")][0:C, 0:HALF * D].rearrange("p (c d) -> p c d", d=D),
                                          h_kept[:, cs, :], ALU.add).then_inc(read[f"o{k}"], 1)

                def norm_stats(src, st, st_done, mo, mo_step, no):
                    for c in range(NC):
                        i = dve.bn_stats(st[:, c, :], src[:, c, :])
                    i.then_inc(st_done, 1)
                    dve.wait_ge(consts_in, 16 * 10)
                    dve.wait_ge(st_done, no + 1)
                    for c in range(NC):
                        i = dve.bn_aggr(mo[:, c, :], st[:, c, :])
                    i.then_inc(mo_step, 1)
                    dve.wait_ge(mo_step, 2 * no + 1)
                    dve.tensor_scalar(mo[:, :, 1], mo[:, :, 1], EPS, None, ALU.add).then_inc(mo_step, 1)

                def normalise(dst, src, mo, r, r_done, done, no):
                    dve.wait_ge(r_done, no + 1)
                    for c in range(NC):
                        i = dve.tensor_scalar(dst[:, c, 0:D], src[:, c, :], mo[:, c, 0:1], r[:, c:c + 1],
                                              ALU.subtract, ALU.mult)
                    i.then_inc(done, 1)

                def projected(unit, k, dst, bias, decay):
                    b = bank_of(unit)
                    dve.wait_ge(filled[unit], after.no + 1)
                    cols = slice(k * HALF * C, (k + 1) * HALF * C)
                    dve.scalar_tensor_tensor(
                        dst[:, cols].rearrange("p (c i) -> p c i", i=C),
                        bank[b][:, 0:HALF * C].rearrange("p (c i) -> p c i", i=C), bias,
                        decay.unsqueeze(1).broadcast_to([128, HALF, C]), ALU.add, ALU.mult).then_inc(read[unit], 1)

                if own:
                    low_scores(5)
                if before:
                    residual()
                if after:
                    if not early(after, 2):
                        dve.wait_ge(filled["a0"], after.no - 1)
                    projected("q0", 0, q_dec[after.slot], w_col[:, 0:1], const("q_decay"))
                if own:
                    low_scores(4)
                    gated_out(5)
                if after:
                    projected("q1", 1, q_dec[after.slot], w_col[:, 0:1], const("q_decay"))
                    for k in range(2):
                        projected(f"k{k}", k, k_dec[after.slot], w_col[:, 1:2], const("k_decay"))
                if own:
                    low_scores(3)
                    gated_out(4)
                if early(own, 1):
                    smooth_part(3)
                if before:
                    dve.wait_ge(read["o1"], before.no + 1)
                    norm_stats(h2_sb[before.slot], stats2, stats2_done, moments2, moments2_step, before.no)
                if own:
                    low_scores(2)
                    gated_out(3)
                if before:
                    if not early(before, 2):
                        dve.wait_ge(rows_out[before.slot], before.pair * 16)
                    normalise(row_sb[before.slot], h2_sb[before.slot], moments2, rstd2, rstd2_done, xn2_done,
                              before.no)
                if after:
                    for k in range(3):
                        dve.wait_ge(filled[f"v{k}"], after.no + 1)
                        dve.tensor_tensor(v_tok[after.slot][:, 2 * k:2 * k + 2, :],
                                          bank[bank_of(f"v{k}")][0:C, 0:2 * D].rearrange("p (c d) -> p c d", c=2),
                                          v_bias[:, :].unsqueeze(1).broadcast_to([C, 2, D]), ALU.add
                                          ).then_inc(read[f"v{k}"], 1)
                if own:
                    low_scores(1)
                    gated_out(2)
                if coming:
                    dve.wait_ge(read["h1"], coming.no + 1)
                    norm_stats(h_sb[coming.slot], stats, stats_done, moments, moments_step, coming.no)
                if after:
                    state_products(0)
                if own:
                    low_scores(0)
                    gated_out(1)
                if coming:
                    if not early(coming, 1):
                        dve.wait_ge(filled["x1"], coming.no)
                    normalise(xn, h_sb[coming.slot], moments, rstd, rstd_done, xn_done, coming.no)
                    if early(coming, 1):
                        smooth_part(2)
                if after:
                    state_products(1)
                    states()
                if before:
                    dve.wait_ge(filled["lg"], before.no + 1)
                    lg = bank[bank_of("lg")][0:C, 0:NC * E].rearrange("p (c e) -> p c e", e=E)
                    dve.tensor_copy(row_sb[before.slot][:, :, D:ROW], lg).then_inc(logits_done, 1)
                    dve.tensor_copy(logits[:, :, bass.ds(before.no * E, E)], lg).then_inc(read["lg"], 1)
                if own:
                    gated_out(0)

            all_steps(dve, step)
        stage1.close()

        def s2(name, shape, dt=F32):
            return ctx.enter_context(nc.sbuf_tensor(name, shape, dt))

        lg_rows = s2("lg_rows", [128, T])
        scratch = s2("scratch", [128, T])
        scratch_part = s2("scratch_part", [128, DVE_PART])
        scratch_act = s2("scratch_act", [128, T])
        scratch_act_part = s2("scratch_act_part", [128, T - DVE_PART])
        row_ends = s2("row_ends", [128, 2])
        ends = s2("ends", [1, 2, E])
        ends_all = s2("ends_all", [128, 2, E])
        ends_sel = s2("ends_sel", [128, 2, E])
        top_low = s2("top_low", [128, 2])
        neg_top = s2("neg_top", [128, 1 + E])
        exp_sum = s2("exp_sum", [128, 1])
        exp_sums = s2("exp_sums", [128, E])
        inv_sum = s2("inv_sum", [128, E])
        low = s2("low", [128, 1])
        width = [s2(f"width{k}", [128, 1]) for k in range(2)]
        thresholds = s2("thresholds", [128, 3])
        counts = s2("counts", [128, 2])
        sign_sums = s2("sign_sums", [128, 2])
        passed = s2("passed", [128, 3])
        n_passed = s2("n_passed", [128, 1])
        high = s2("high", [128, 1])
        sure = s2("sure", [128, T])
        band = s2("band", [128, T])
        offsets = s2("offsets", [128, 2])
        sure_rank = s2("sure_rank", [128, T])
        band_rank = s2("band_rank", [128, T])
        place = s2("place", [128, T])
        place_tok = s2("place_tok", [C, E, TILES], I32)
        block_int = s2("block_int", [C, E, TILES], I32)
        slot_int = s2("slot_int", [C, E, TILES], I32)
        block16 = s2("block16", [C, E, TILES], BF16)
        slot16 = s2("slot16", [C, E, TILES], BF16)
        slot_hot = [s2(f"slot_hot{k}", [C, RUNS, 128, RUN], BF16) for k in range(2)]
        block_hot = s2("block_hot", [C, RUNS, G, RUN], BF16)
        block_val = [s2(f"block_val{k}", [C, RUNS, 2 * G, RUN], BF16) for k in range(2)]
        carrier = s2("carrier", [1, 1])
        idx_tile = s2("idx_tile", [128, G])
        idx = [s2(f"idx{k}", [128, G], U32) for k in range(2)]
        idx_add = [s2(f"idx_add{k}", [128, G], U32) for k in range(2)]
        taken = [s2(f"taken{k}", [128, G, ROW]) for k in range(2)]
        takenT = s2("takenT", [D, CAP])
        hidden = s2("hidden", [128, FT, CAP])
        weight_exp = s2("weight_exp", [128, G])
        weight = s2("weight", [128, G])
        y_sum = s2("y_sum", [128, G, D])
        y = [s2(f"y{k}", [128, G, D]) for k in range(2)]
        w1_sb = [s2(f"w1_sb{k}", [D, F]) for k in range(2)]
        w2_sb = [s2(f"w2_sb{k}", [128, FT, D]) for k in range(2)]
        b1_sb = [s2(f"b1_sb{k}", [128, FT]) for k in range(2)]
        b2_sb = [s2(f"b2_sb{k}", [128, D]) for k in range(2)]

        banks = [psum(f"bank2_{k}", [128, 512]) for k in range(8)]
        ps_idx, ps_T, ps_H, ps_Y = banks[0], banks[1:3], banks[3:6], banks[6:8]

        turned = sem("turned")
        lg_copied = sem("lg_copied")
        dve_step = sem("dve_step")
        ends_turned = sem("ends_turned")
        ends_done = sem("ends_done")
        ends_spread = sem("ends_spread")
        top_done = sem("top_done")
        exp_done = sem("exp_done")
        exp_sums_done = sem("exp_sums_done")
        sums_spread = sem("sums_spread")
        inverse_done = sem("inverse_done")
        thresholds_set = sem("thresholds_set")
        counted_dve = sem("counted_dve")
        counted_act = sem("counted_act")
        totals_done = sem("totals_done")
        round_step = sem("round_step")
        rows_ranked = sem("rows_ranked")
        offsets_done = sem("offsets_done")
        place_done = sem("place_done")
        place_turned = sem("place_turned")
        split_step = sem("split_step")
        hot_step = sem("hot_step")
        hot_done = sem("hot_done")
        idx_ps = sem("idx_ps")
        idx_step = sem("idx_step")
        carried = sem("carried")
        idx_done = sem("idx_done")
        idx_kept = sem("idx_kept")
        taken_in = [[sem(f"taken_in{k}_{half}") for half in range(2)] for k in range(2)]
        taken_turned = sem("taken_turned")
        takenT_done = sem("takenT_done")
        hidden_ps = sem("hidden_ps")
        hidden_done = sem("hidden_done")
        weight_step = sem("weight_step")
        weight_done = sem("weight_done")
        y_ps = sem("y_ps")
        y_step = sem("y_step")
        y_done = sem("y_done")
        added = [sem(f"added{k}") for k in range(2)]
        weights_in = [sem(f"weights_in{k}") for k in range(2)]

        block = ctx.enter_context(nc.Block())

        def all_experts(eng, step):
            step(item(0), False)
            step(item(1), False)
            with eng.Fori(1, E // 2 - 1) as i:
                step(Item(i * 2, i, 0), False)
                step(Item(i * 2 + 1, i, 1), False)
            step(item(E - 2), True)
            step(item(E - 1), True)

        @block.sync
        def _(sp):
            def load(it):
                one = bass.ds(it.no, 1)
                got = weights_in[it.slot]
                if not early(it, 2):
                    sp.wait_ge(hidden_done, 8 * (it.no - 1))
                sp.dma_start(w1_sb[it.slot][:, :], w1[one].rearrange("a d f -> (a d) f")).then_inc(got, 16)
                sp.dma_start(b1_sb[it.slot][:, :], b1[one].rearrange("a (p t) -> (a p) t", t=FT)).then_inc(got, 16)
                if not early(it, 2):
                    sp.wait_ge(y_ps, 2 * (it.no - 1))
                sp.dma_start(w2_sb[it.slot][:, :, :], w2[one].rearrange("a (p t) d -> (a p) t d", t=FT)).then_inc(got, 16)
                if not early(it, 2):
                    sp.wait_ge(y_done, 2 * (it.no - 1))
                sp.dma_start(b2_sb[it.slot][:, :], b2[one].broadcast_to([128, D])).then_inc(got, 16)

            load(item(0))
            load(item(1))
            with sp.Fori(1, E // 2) as i:
                load(Item(i * 2, i, 0))
                load(Item(i * 2 + 1, i, 1))

        @block.tensor
        def _(pe):
            for c in range(NC):
                m = pe.transpose(banks[c // HALF][:, chunk(c % HALF)], logits[:, c, :], ident[0:C, 0:C])
                if c % HALF == HALF - 1:
                    m.then_inc(turned, 1)
            pe.wait_ge(dve_step, 2)
            for k in range(2):
                m = pe.transpose(banks[2][0:1, k * 128:(k + 1) * 128], row_ends[:, k:k + 1], ident)
            m.then_inc(ends_turned, 1)
            pe.wait_ge(ends_done, 2)
            pe.matmul(banks[3][:, 0:2 * E], const("ones")[0:1, :], ends[:, :, :].rearrange("p k e -> p (k e)"),
                      start=True, stop=True).then_inc(ends_spread, 1)
            with pe.Fori(0, ROUNDS // UNROLL) as i:
                for j in range(UNROLL):
                    r = i * UNROLL + j
                    pe.wait_ge(thresholds_set, r + 1)
                    pe.matmul(banks[5][:, 0:3], const("same_expert"), const("sign_base"), start=True, stop=False,
                              skip_group_check=True)
                    pe.wait_ge(counted_act, r + 1)
                    pe.matmul(banks[5][:, 1:3], const("same_expert"), sign_sums[:, :], start=False, stop=False,
                              skip_group_check=True)
                    pe.wait_ge(counted_dve, r + 1)
                    pe.matmul(banks[5][:, 0:2], const("same_twice"), counts[:, :], start=False, stop=True,
                              skip_group_check=True).then_inc(totals_done, 1)
            pe.wait_ge(rows_ranked, 1)
            pe.matmul(banks[4][:, 0:1], const("earlier_row"), sure_rank[:, T - 1:T], start=True, stop=True)
            pe.matmul(banks[4][:, 1:2], const("earlier_row"), band_rank[:, T - 1:T], start=True, stop=False,
                      skip_group_check=True)
            pe.matmul(banks[4][:, 1:2], const("same_expert"), sure_rank[:, T - 1:T], start=False, stop=True,
                      skip_group_check=True).then_inc(offsets_done, 1)
            pe.wait_ge(place_done, 1)
            for c in range(NC):
                m = pe.transpose(banks[6 + c // 4][0:C, (c % 4) * 128:(c % 4 + 1) * 128], place[:, chunk(c)], ident)
                if c in (3, NC - 1):
                    m.then_inc(place_turned, 1)

            def index(it):
                pe.wait_ge(hot_done, it.no + 1)
                pe.wait_ge(idx_done, it.no)
                for t in range(TILES):
                    m = pe.matmul(ps_idx[:, 0:2 * G], slot_hot[it.slot][:, t // RUN, :, t % RUN],
                                  block_val[it.slot][:, t // RUN, :, t % RUN],
                                  start=(t == 0), stop=(t == TILES - 1))
                m.then_inc(idx_ps, 1)

            index(item(0))
            pe.wait_ge(exp_sums_done, 1)
            pe.matmul(banks[4][:, 0:E], const("ones"), exp_sums[:, :], start=True, stop=True).then_inc(sums_spread, 1)
            pe.wait_ge(inverse_done, 1)

            def step(it, last):
                def turn(k):
                    pe.wait_ge(taken_in[it.slot][k], it.pair * 64 + 64)
                    pe.wait_ge(takenT_done, it.no * 2)
                    for g in range(4):
                        m = pe.transpose(ps_T[k][:, g * 128:(g + 1) * 128], taken[it.slot][:, 4 * k + g, 0:D], ident)
                    m.then_inc(taken_turned, 1)

                turn(0)
                if not (last and it.slot == 1):
                    index(Item(it.no + 1, it.pair + it.slot, 1 - it.slot))
                pe.wait_ge(weights_in[it.slot], it.pair * 64 + 64)
                for u in range(2 * FT):
                    k, f = u // FT, u % FT
                    if u == 2:
                        turn(1)
                    if f == 0:
                        pe.wait_ge(takenT_done, it.no * 2 + k + 1)
                    pe.wait_ge(hidden_done, it.no * 8 + max(u - 2, 0))
                    pe.matmul(ps_H[u % 3][:, :], w1_sb[it.slot][:, f * 128:(f + 1) * 128],
                              takenT[:, k * 512:(k + 1) * 512], start=True, stop=True).then_inc(hidden_ps, 1)
                for g in range(G):
                    if g % 4 == 0:
                        pe.wait_ge(hidden_done, it.no * 8 + 4 + g)
                        pe.wait_ge(y_done, it.no * 2)
                    for f in range(FT):
                        m = pe.matmul(ps_Y[g // 4][:, (g % 4) * D:(g % 4 + 1) * D],
                                      hidden[:, f, g * 128:(g + 1) * 128], w2_sb[it.slot][:, f, :],
                                      start=(f == 0), stop=(f == FT - 1), skip_group_check=True)
                    if g % 4 == 3:
                        m.then_inc(y_ps, 1)

            all_experts(pe, step)

        @block.scalar
        def _(act):
            with act.Fori(0, ROUNDS // UNROLL) as i:
                for j in range(UNROLL):
                    r = i * UNROLL + j
                    act.wait_ge(thresholds_set, r + 1)
                    act.activation(scratch_act[:, :], lg_rows[:, :], ACT.Sign, bias=thresholds[:, 2:3], scale=-1.0,
                                   accum_out=sign_sums[:, 1:2])
                    act.activation(scratch_act_part[:, :], lg_rows[:, DVE_PART:T], ACT.Sign, bias=thresholds[:, 1:2],
                                   scale=-1.0, accum_out=sign_sums[:, 0:1]).then_inc(counted_act, 1)
            act.wait_ge(top_done, 1)
            act.wait_ge(counted_act, ROUNDS)
            act.activation(scratch_act[:, :], lg_rows[:, :], ACT.Exp, bias=neg_top[:, 0:1],
                           accum_out=exp_sum[:, :]).then_inc(exp_done, 1)

            def weights_of(it):
                for half in range(2):
                    act.wait_ge(taken_in[it.slot][half], it.pair * 64 + 64)
                act.wait_ge(weight_done, it.no)
                act.activation(weight_exp[:, :], taken[it.slot][:, :, bass.ds(it.no + D, 1)].rearrange("p g a -> p (g a)"),
                               ACT.Exp, bias=neg_top[:, bass.ds(it.no + 1, 1)]).then_inc(weight_step, 1)

            def step(it, last):
                def copy_turned(k):
                    act.wait_ge(taken_turned, it.no * 2 + k + 1)
                    act.wait_ge(hidden_ps, it.no * 8)
                    act.copy(takenT[:, k * 512:(k + 1) * 512], ps_T[k][:, :]).then_inc(takenT_done, 1)

                copy_turned(0)
                act.wait_ge(weights_in[it.slot], it.pair * 64 + 64)
                act.wait_ge(y_ps, it.no * 2)
                for u in range(2 * FT):
                    if u == 2:
                        copy_turned(1)
                    act.wait_ge(hidden_ps, it.no * 8 + u + 1)
                    k, f = u // FT, u % FT
                    act.activation(hidden[:, f, k * 512:(k + 1) * 512], ps_H[u % 3][:, :], ACT.Gelu,
                                   bias=b1_sb[it.slot][:, f:f + 1]).then_inc(hidden_done, 1)
                if early(it, 1):
                    weights_of(it)
                if not (last and it.slot == 1):
                    weights_of(Item(it.no + 1, it.pair + it.slot, 1 - it.slot))

            all_experts(act, step)

        @block.gpsimd
        def _(pool):
            last_token = pool.to_reg(N - 1)

            def carry_waits(count):
                pool.wait_ge(carried, count)
                pool.tensor_tensor(carrier[:, :], const("ones")[0:1, 0:1], const("ones")[0:1, 0:1],
                                   ALU.mult).then_inc(carried, 1)

            def take(it):
                pool.wait_ge(idx_done, it.no + 1)
                if not early(it, 2):
                    pool.wait_ge(taken_turned, it.no * 2 - 2)
                    pool.wait_ge(weight_step, it.no - 1)
                carry_waits(0 if early(it, 1) else it.no * 3 - 2)
                for g in range(G):
                    pool.indirect_dma_start(
                        out=taken[it.slot][:, g, :], out_offset=None, in_=rows_dram[:, :],
                        in_offset=bass.IndirectOffsetOnAxis(ap=idx[it.slot][:, g:g + 1], axis=0),
                        bounds_check=last_token, oob_is_err=False).then_inc(taken_in[it.slot][g // 4], 16)

            for k in range(2):
                pool.wait_ge(rows_out[k], 16 * B // 2)
                pool.wait_ge(h2_out[k], 16 * B // 2)
            take(item(0))

            def step(it, last):
                if not (last and it.slot == 1):
                    after = Item(it.no + 1, it.pair + it.slot, 1 - it.slot)
                    take(after)
                for k in range(2):
                    pool.wait_ge(y_done, it.no * 2 + k + 1)
                    if k == 0:
                        pool.wait_ge(added[1 - it.slot], (it.pair + it.slot) * 128)
                    carry_waits(it.no * 3 + k + (1 if last and it.slot == 1 else 2))
                    for g in range(4 * k, 4 * k + 4):
                        pool.indirect_dma_start(
                            out=out_rows[:, :], out_offset=bass.IndirectOffsetOnAxis(ap=idx_add[it.slot][:, g:g + 1], axis=0),
                            in_=y[it.slot][:, g, :], in_offset=None, bounds_check=last_token, oob_is_err=True,
                            compute_op=ALU.add).then_inc(added[it.slot], 16)

            all_experts(pool, step)
            for k in range(2):
                pool.wait_ge(added[k], E // 2 * 128)

        @block.vector
        def _(dve):
            dve.tensor_copy(numbers16[:, :], const("numbers"))
            for k in range(2):
                dve.wait_ge(turned, k + 1)
                dve.tensor_copy(lg_rows[:, k * HALF * C:(k + 1) * HALF * C], banks[k][:, 0:HALF * C]
                                ).then_inc(lg_copied, 1)
            dve.wait_ge(lg_copied, 2)
            dve.tensor_reduce(row_ends[:, 0:1], lg_rows[:, :], AX_X, ALU.max).then_inc(dve_step, 1)
            dve.tensor_reduce(row_ends[:, 1:2], lg_rows[:, :], AX_X, ALU.min).then_inc(dve_step, 1)
            dve.wait_ge(ends_turned, 1)
            for k, op in enumerate((ALU.max, ALU.min)):
                dve.tensor_reduce(ends[:, k, :], banks[2][0:1, k * 128:(k + 1) * 128].rearrange("p (b e) -> p e b", e=E),
                                  AX_X, op).then_inc(ends_done, 1)
            dve.wait_ge(ends_spread, 1)
            dve.tensor_copy(ends_all[:, :, :].rearrange("p k e -> p (k e)"), banks[3][:, 0:2 * E]).then_inc(dve_step, 1)
            dve.wait_ge(dve_step, 3)
            dve.tensor_tensor(ends_sel[:, :, :], ends_all[:, :, :],
                              const("expert_of").unsqueeze(1).broadcast_to([128, 2, E]), ALU.mult).then_inc(dve_step, 1)
            dve.tensor_scalar(neg_top[:, 1:1 + E], ends_all[:, 0, :], -1.0, None, ALU.mult)
            dve.wait_ge(dve_step, 4)
            dve.tensor_reduce(top_low[:, :], ends_sel[:, :, :], AX_X, ALU.add).then_inc(dve_step, 1)
            dve.wait_ge(dve_step, 5)
            dve.tensor_scalar(neg_top[:, 0:1], top_low[:, 0:1], -1.0, None, ALU.mult).then_inc(top_done, 1)
            dve.tensor_tensor(width[1][:, :], top_low[:, 0:1], top_low[:, 1:2], ALU.subtract).then_inc(dve_step, 1)
            dve.tensor_copy(low[:, :], top_low[:, 1:2])
            dve.wait_ge(dve_step, 6)
            dve.tensor_scalar(width[0][:, :], width[1][:, :], 0.25, None, ALU.mult).then_inc(dve_step, 1)
            dve.wait_ge(dve_step, 7)

            def next_thresholds(w):
                return dve.scalar_tensor_tensor(thresholds[:, :], const("k_of"), w[:, 0:1],
                                                low[:, 0:1].broadcast_to([128, 3]), ALU.mult, ALU.add)

            next_thresholds(width[0]).then_inc(thresholds_set, 1)
            with dve.Fori(0, ROUNDS // UNROLL) as i:
                for j in range(UNROLL):
                    r = i * UNROLL + j
                    now, narrower = width[j % 2], width[1 - j % 2]
                    dve.wait_ge(thresholds_set, r + 1)
                    dve.tensor_scalar(scratch[:, :], lg_rows[:, :], thresholds[:, 0:1], None, ALU.is_lt, ALU.add,
                                      accum_out=counts[:, 0:1])
                    dve.tensor_scalar(scratch_part[:, :], lg_rows[:, 0:DVE_PART], thresholds[:, 1:2], None, ALU.is_lt,
                                      ALU.add, accum_out=counts[:, 1:2]).then_inc(counted_dve, 1)
                    dve.tensor_scalar(narrower[:, :], now[:, :], 0.25, None, ALU.mult)
                    dve.wait_ge(totals_done, r + 1)
                    dve.tensor_scalar(passed[:, :], banks[5][:, 0:3], float(2 * (N - CAP)), None, ALU.is_le, ALU.add,
                                      accum_out=n_passed[:, :]).then_inc(round_step, 1)
                    dve.wait_ge(round_step, r * 2 + 1)
                    dve.scalar_tensor_tensor(low[:, :], n_passed[:, :], now[:, 0:1], low[:, :], ALU.mult,
                                             ALU.add).then_inc(round_step, 1)
                    dve.wait_ge(round_step, r * 2 + 2)
                    next_thresholds(narrower).then_inc(thresholds_set, 1)
            dve.scalar_tensor_tensor(high[:, :], width[0][:, :], 4.0, low[:, :], ALU.mult, ALU.add).then_inc(dve_step, 1)
            dve.wait_ge(dve_step, 8)
            dve.tensor_scalar(sure[:, :], lg_rows[:, :], high[:, 0:1], None, ALU.is_gt).then_inc(dve_step, 1)
            dve.wait_ge(dve_step, 9)
            dve.scalar_tensor_tensor(band[:, :], lg_rows[:, :], low[:, 0:1], sure[:, :], ALU.is_ge,
                                     ALU.subtract).then_inc(dve_step, 1)
            ones = const("ones")[:, 0:1].broadcast_to([128, T])
            dve.tensor_tensor_scan(sure_rank[:, :], ones, sure[:, :], 0.0, ALU.mult, ALU.add)
            dve.wait_ge(dve_step, 10)
            dve.tensor_tensor_scan(band_rank[:, :], ones, band[:, :], 0.0, ALU.mult, ALU.add).then_inc(rows_ranked, 1)
            dve.wait_ge(offsets_done, 1)
            dve.tensor_copy(offsets[:, :], banks[4][:, 0:2]).then_inc(dve_step, 1)
            dve.wait_ge(dve_step, 11)
            dve.scalar_tensor_tensor(sure_rank[:, :], sure_rank[:, :], offsets[:, 0:1], sure[:, :], ALU.add, ALU.mult)
            dve.scalar_tensor_tensor(band_rank[:, :], band_rank[:, :], offsets[:, 1:2], band[:, :], ALU.add,
                                     ALU.mult).then_inc(dve_step, 1)
            dve.wait_ge(dve_step, 12)
            dve.scalar_tensor_tensor(place[:, :], sure_rank[:, :], -1.0, band_rank[:, :], ALU.add,
                                     ALU.add).then_inc(place_done, 1)

            def split_places(lo, hi, step):
                for k, (first, last) in enumerate(((0, 4), (4, NC))):
                    dve.wait_ge(place_turned, k + 1)
                    dve.tensor_copy(place_tok[:, lo:hi, first * B:last * B],
                                    banks[6 + k][0:C, 0:(last - first) * 128].rearrange("p (t e) -> p e t", e=E)[:, lo:hi, :]
                                    ).then_inc(split_step, 1)
                mine = slice(lo, hi)
                dve.wait_ge(split_step, step + 2)
                dve.tensor_scalar(block_int[:, mine, :], place_tok[:, mine, :], 7, None, ALU.arith_shift_right)
                dve.tensor_scalar(slot_int[:, mine, :], place_tok[:, mine, :], 127, None,
                                  ALU.bitwise_and).then_inc(split_step, 1)
                dve.wait_ge(split_step, step + 3)
                dve.tensor_copy(block16[:, mine, :], block_int[:, mine, :])
                dve.tensor_copy(slot16[:, mine, :], slot_int[:, mine, :]).then_inc(split_step, 1)
                dve.wait_ge(split_step, step + 4)

            at = 128 * RUN
            slot_nos = numbers16[0:C, 0:at].rearrange("p (s t) -> p s t", t=RUN).unsqueeze(1)
            block_nos = numbers16[0:C, at:at + G * RUN].rearrange("p (s t) -> p s t", t=RUN).unsqueeze(1)
            at += G * RUN
            tile_nos = numbers16[0:C, at:at + TILES].rearrange("p (u t) -> p u t", t=RUN).unsqueeze(2)

            def hot(it):
                if not early(it, 2):
                    dve.wait_ge(idx_ps, it.no - 1)
                mine = bass.ds(it.no, 1)
                slots = slot16[:, mine, :].rearrange("p a (u t) -> p (a u) t", t=RUN).unsqueeze(2)
                blocks = block16[:, mine, :].rearrange("p a (u t) -> p (a u) t", t=RUN).unsqueeze(2)
                dve.tensor_tensor(slot_hot[it.slot][:, :, :, :], slot_nos.broadcast_to([C, RUNS, 128, RUN]),
                                  slots.broadcast_to([C, RUNS, 128, RUN]), ALU.is_equal)
                dve.wait_ge(hot_done, it.no)
                dve.tensor_tensor(block_hot[:, :, :, :], block_nos.broadcast_to([C, RUNS, G, RUN]),
                                  blocks.broadcast_to([C, RUNS, G, RUN]), ALU.is_equal).then_inc(hot_step, 1)
                dve.wait_ge(hot_step, it.no + 1)
                dve.tensor_scalar(block_val[it.slot][:, :, 0:G, :], block_hot[:, :, :, :], const("partition", C), None,
                                  ALU.mult)
                dve.tensor_tensor(block_val[it.slot][:, :, G:2 * G, :], block_hot[:, :, :, :],
                                  tile_nos.broadcast_to([C, RUNS, G, RUN]), ALU.mult).then_inc(hot_done, 1)

            def list_out(it):
                dve.wait_ge(idx_ps, it.no + 1)
                dve.tensor_scalar(idx_tile[:, :], ps_idx[:, G:2 * G], float(C), None, ALU.mult).then_inc(idx_step, 1)
                if not early(it, 2):
                    for half in range(2):
                        dve.wait_ge(taken_in[it.slot][half], it.pair * 64)
                    dve.wait_ge(idx_kept, it.no - 1)
                dve.wait_ge(idx_step, it.no + 1)
                dve.tensor_tensor(idx[it.slot][:, :], idx_tile[:, :], ps_idx[:, 0:G], ALU.add).then_inc(idx_done, 1)

            split_places(0, 1, 0)
            hot(item(0))
            split_places(1, E, 4)
            dve.wait_ge(exp_done, 1)
            dve.tensor_scalar(exp_sums[:, :], const("expert_of"), exp_sum[:, 0:1], None, ALU.mult).then_inc(exp_sums_done, 1)
            list_out(item(0))
            dve.wait_ge(sums_spread, 1)
            dve.reciprocal(inv_sum[:, :], banks[4][:, 0:E]).then_inc(inverse_done, 1)
            hot(item(1))

            def step(it, last):
                if not (last and it.slot == 1):
                    after = Item(it.no + 1, it.pair + it.slot, 1 - it.slot)
                    list_out(after)
                if not last:
                    hot(Item(it.no + 2, it.pair + 1, it.slot))
                dve.wait_ge(y_done, it.no * 2)
                dve.wait_ge(weight_step, it.no + 1)
                dve.tensor_scalar(weight[:, :], weight_exp[:, :], inv_sum[:, bass.ds(it.no, 1)], None,
                                  ALU.mult).then_inc(weight_done, 1)
                if not early(it, 2):
                    dve.wait_ge(added[it.slot], it.pair * 128)
                dve.wait_ge(idx_done, it.no + 1)
                dve.tensor_copy(idx_add[it.slot][:, :], idx[it.slot][:, :]).then_inc(idx_kept, 1)
                for k in range(2):
                    dve.wait_ge(y_ps, it.no * 2 + k + 1)
                    dve.tensor_tensor(y_sum[:, 4 * k:4 * k + 4, :], ps_Y[k][:, :].rearrange("p (g d) -> p g d", d=D),
                                      b2_sb[it.slot][:, :].unsqueeze(1).broadcast_to([128, 4, D]), ALU.add
                                      ).then_inc(y_step, 1)
                    dve.wait_ge(y_step, it.no * 2 + k + 1)
                    dve.tensor_tensor(y[it.slot][:, 4 * k:4 * k + 4, :], y_sum[:, 4 * k:4 * k + 4, :],
                                      weight[:, 4 * k:4 * k + 4].unsqueeze(2).broadcast_to([128, 4, D]), ALU.mult
                                      ).then_inc(y_done, 1)

            all_experts(dve, step)


_INS = ["x", "L0_tok_W_ve", "L0_tok_b_ve", "L0_tok_W_lin", "L0_tok_b_lin", "L0_attn_wq", "L0_attn_bq", "L0_attn_wk",
        "L0_attn_bk", "L0_attn_wv", "L0_attn_bv", "L0_attn_wg", "L0_attn_bg", "L0_ffn_Wr", "L0_ffn_W1", "L0_ffn_b1",
        "L0_ffn_W2", "L0_ffn_b2"]


def kernel(**inputs):
    import concourse.bacc as bacc
    from concourse.bass_utils import run_bass_kernel_spmd

    nc = bacc.Bacc("TRN2", target_bir_lowering=False, num_devices=1)
    data = {name: np.ascontiguousarray(inputs[name]) for name in _INS}
    data["L0_ffn_W1"] = np.ascontiguousarray(
        data["L0_ffn_W1"].reshape(E, D, 128, FT).transpose(0, 1, 3, 2).reshape(E, D, F))
    data["consts"] = constants()
    arrays, args = {}, []
    for name, a in data.items():
        arrays[f"in_{name}"] = a
        args.append(nc.dram_tensor(f"in_{name}", a.shape, mybir.dt.from_np(a.dtype), kind="ExternalInput").ap())
    args.append(nc.dram_tensor("out", (B, T, D), F32, kind="ExternalOutput").ap())
    program(nc, *args)
    r = run_bass_kernel_spmd(nc, [arrays], core_ids=[0])
    return r.results[0]["out"]
```
